# Optimizing a Trainium2 kernel written in Bass

```python
import numpy as np
import jax
import jax.numpy as jnp

def _softmax(x, axis=-1):
    return jax.nn.softmax(x, axis=axis)

def _gelu(x):
    return jax.nn.gelu(x, approximate=True)

def _silu(x):
    return jax.nn.silu(x)

def _sigmoid(x):
    return jax.nn.sigmoid(x)

def _layernorm(x, axis=-1, eps=1e-05):
    m = jnp.mean(x, axis=axis, keepdims=True)
    v = jnp.var(x, axis=axis, keepdims=True)
    return (x - m) / jnp.sqrt(v + eps)

def _scatter_add(tgt, idx, src, axis=0):
    return tgt.at[idx].add(src)

def _segment_sum(src, seg, n):
    return jax.ops.segment_sum(src, seg, n)
kernel_name = 'mk_sandwich_d2_jaxref_r4_825681'

def setup_inputs(seed: int=0):
    np.random.seed(seed)
    _w = jnp.asarray

    def _L0_attn_setup():
        import jax, jax.numpy as jnp
        import numpy as np
        B, S, D = (2, 1024, 512)
        H, HKV, DH = (16, 4, 128)
        CHUNK = 64
        GROUPS = H // HKV

        def _alibi_slopes(n_heads):
            i = jnp.arange(1, n_heads + 1, dtype=jnp.float32)
            return jnp.exp2(-8.0 * i / n_heads)

        def _rope(x):
            s, d = (x.shape[2], x.shape[3])
            inv_freq = 1.0 / 10000.0 ** (jnp.arange(0, d, 2, dtype=jnp.float32) / d)
            freqs = jnp.arange(s, dtype=jnp.float32)[:, None] * inv_freq[None, :]
            cos = jnp.concatenate([jnp.cos(freqs), jnp.cos(freqs)], axis=-1)
            sin = jnp.concatenate([jnp.sin(freqs), jnp.sin(freqs)], axis=-1)
            x1, x2 = (x[..., :d // 2], x[..., d // 2:])
            rot = jnp.concatenate([-x2, x1], axis=-1)
            return x * cos[None, None] + rot * sin[None, None]

        def _lightning_attn(q, k, v):
            b, h, s, dh = q.shape
            nc = s // CHUNK
            lam = _alibi_slopes(h)
            r = jnp.arange(CHUNK, dtype=jnp.float32)
            diff = r[:, None] - r[None, :]
            diag = jnp.where(diff >= 0, jnp.exp(-lam[:, None, None] * diff), 0.0)
            q_dec = jnp.exp(-lam[:, None] * (r + 1.0))
            k_dec = jnp.exp(-lam[:, None] * (CHUNK - 1.0 - r))
            blk = jnp.exp(-lam * CHUNK)
            qc = q.reshape(b, h, nc, CHUNK, dh).transpose(2, 0, 1, 3, 4)
            kc = k.reshape(b, h, nc, CHUNK, dh).transpose(2, 0, 1, 3, 4)
            vc = v.reshape(b, h, nc, CHUNK, dh).transpose(2, 0, 1, 3, 4)

            def step(kv, inp):
                qi, ki, vi = inp
                scores = jnp.einsum('bhid,bhjd->bhij', qi, ki) * diag[None]
                o_intra = jnp.einsum('bhij,bhje->bhie', scores, vi)
                o_inter = jnp.einsum('bhid,bhde->bhie', qi * q_dec[None, :, :, None], kv)
                kv = blk[None, :, None, None] * kv + jnp.einsum('bhjd,bhje->bhde', ki * k_dec[None, :, :, None], vi)
                return (kv, o_intra + o_inter)
            kv0 = jnp.zeros((b, h, dh, dh), q.dtype)
            _, o = jax.lax.scan(step, kv0, (qc, kc, vc))
            return o.transpose(1, 2, 0, 3, 4).reshape(b, h, s, dh)
        key = jax.random.key(seed)
        ks = jax.random.split(key, 5)
        sc = 0.02
        return {'x': jax.random.normal(ks[0], (B, S, D), jnp.float32), 'wq': jax.random.normal(ks[1], (H * DH, D), jnp.float32) * sc, 'wk': jax.random.normal(ks[2], (HKV * DH, D), jnp.float32) * sc, 'wv': jax.random.normal(ks[3], (HKV * DH, D), jnp.float32) * sc, 'wo': jax.random.normal(ks[4], (D, H * DH), jnp.float32) * sc}
    _L0_attn_in = _L0_attn_setup()

    def _L0_ffn_setup():
        import jax, jax.numpy as jnp
        import numpy as np
        ZERO_POINT = 128.0

        def _dequant(wq, scale):
            return (wq.astype(jnp.float32) - ZERO_POINT) * scale[:, None]
        key = jax.random.key(seed)
        ks = jax.random.split(key, 7)
        H, I = (512, 2048)
        B, S = (2, 512)
        hidden_state = jax.random.normal(ks[0], (B, S, H), dtype=jnp.float32)
        gate_w = jax.random.randint(ks[1], (I, H), 0, 64, dtype=jnp.int32)
        up_w = jax.random.randint(ks[2], (I, H), 0, 64, dtype=jnp.int32)
        down_w = jax.random.randint(ks[3], (H, I), 0, 64, dtype=jnp.int32)
        gate_scale = jax.random.uniform(ks[4], (I,), dtype=jnp.float32) * 0.02
        up_scale = jax.random.uniform(ks[5], (I,), dtype=jnp.float32) * 0.02
        down_scale = jax.random.uniform(ks[6], (H,), dtype=jnp.float32) * 0.02
        return {'hidden_state': hidden_state, 'gate_w': gate_w, 'gate_scale': gate_scale, 'up_w': up_w, 'up_scale': up_scale, 'down_w': down_w, 'down_scale': down_scale}
    _L0_ffn_in = _L0_ffn_setup()

    def _L1_attn_setup():
        import jax, jax.numpy as jnp
        import numpy as np
        import math
        D = 512
        H = 32
        HKV = 8
        HD = D // H
        ROPE_BASE = 10000.0

        def _rope_cache(T, hd, base=ROPE_BASE):
            theta = 1.0 / base ** (jnp.arange(0, hd, 2, dtype=jnp.float32) / hd)
            t = jnp.arange(T, dtype=jnp.float32)
            freqs = t[:, None] * theta[None, :]
            return (jnp.cos(freqs), jnp.sin(freqs))

        def _apply_rope(x, cos, sin):
            B, Hh, T, hd = x.shape
            x_ = x.reshape(B, Hh, T, hd // 2, 2)
            x1, x2 = (x_[..., 0], x_[..., 1])
            c = cos[None, None, :, :]
            s = sin[None, None, :, :]
            rx1 = x1 * c - x2 * s
            rx2 = x1 * s + x2 * c
            return jnp.stack([rx1, rx2], axis=-1).reshape(B, Hh, T, hd)
        key = jax.random.key(seed)
        ks = jax.random.split(key, 5)
        B, T = (1, 512)
        sc = 0.02
        return {'x': jax.random.normal(ks[0], (B, T, D), dtype=jnp.float32), 'wq': jax.random.normal(ks[1], (D, D), dtype=jnp.float32) * sc, 'wk': jax.random.normal(ks[2], (HKV * HD, D), dtype=jnp.float32) * sc, 'wv': jax.random.normal(ks[3], (HKV * HD, D), dtype=jnp.float32) * sc, 'wo': jax.random.normal(ks[4], (D, D), dtype=jnp.float32) * sc}
    _L1_attn_in = _L1_attn_setup()

    def _L1_ffn_setup():
        import jax, jax.numpy as jnp
        import numpy as np
        EPS = 1e-06
        K_STEPS = 4
        USE_GATING = True

        def layer_norm(x, gamma, beta):
            mu = jnp.mean(x, axis=-1, keepdims=True)
            var = jnp.mean(jnp.square(x - mu), axis=-1, keepdims=True)
            return (x - mu) * jax.lax.rsqrt(var + EPS) * gamma + beta
        key = jax.random.key(seed)
        B, L, D, H = (4, 1024, 512, 2048)
        ks = jax.random.split(key, 16)
        s = 0.02
        return {'x': jax.random.normal(ks[0], (B, L, D), dtype=jnp.float32), 'in_gamma': jnp.ones((D,), jnp.float32), 'in_beta': jnp.zeros((D,), jnp.float32), 'agg_w': jax.random.normal(ks[1], (D, D), jnp.float32) * s, 'agg_b': jnp.zeros((D,), jnp.float32), 'pn_gamma': jnp.ones((D,), jnp.float32), 'pn_beta': jnp.zeros((D,), jnp.float32), 'd1_w': jax.random.normal(ks[2], (D, H), jnp.float32) * s, 'd1_b': jnp.zeros((H,), jnp.float32), 'd2_w': jax.random.normal(ks[3], (H, D), jnp.float32) * s, 'd2_b': jnp.zeros((D,), jnp.float32), 'bc_w': jax.random.normal(ks[4], (D, D), jnp.float32) * s, 'bc_b': jnp.zeros((D,), jnp.float32), 'gate_w': jax.random.normal(ks[5], (D, D), jnp.float32) * s, 'gate_b': jnp.zeros((D,), jnp.float32), 'out_gamma': jnp.ones((D,), jnp.float32), 'out_beta': jnp.zeros((D,), jnp.float32)}
    _L1_ffn_in = _L1_ffn_setup()
    _d = {'L0_attn_x': _L0_attn_in['x'], 'L0_attn_wq': _L0_attn_in['wq'], 'L0_attn_wk': _L0_attn_in['wk'], 'L0_attn_wv': _L0_attn_in['wv'], 'L0_attn_wo': _L0_attn_in['wo'], 'L0_ffn_gate_w': _L0_ffn_in['gate_w'], 'L0_ffn_gate_scale': _L0_ffn_in['gate_scale'], 'L0_ffn_up_w': _L0_ffn_in['up_w'], 'L0_ffn_up_scale': _L0_ffn_in['up_scale'], 'L0_ffn_down_w': _L0_ffn_in['down_w'], 'L0_ffn_down_scale': _L0_ffn_in['down_scale'], 'L1_attn_wq': _L1_attn_in['wq'], 'L1_attn_wk': _L1_attn_in['wk'], 'L1_attn_wv': _L1_attn_in['wv'], 'L1_attn_wo': _L1_attn_in['wo'], 'L1_ffn_in_gamma': _L1_ffn_in['in_gamma'], 'L1_ffn_in_beta': _L1_ffn_in['in_beta'], 'L1_ffn_agg_w': _L1_ffn_in['agg_w'], 'L1_ffn_agg_b': _L1_ffn_in['agg_b'], 'L1_ffn_pn_gamma': _L1_ffn_in['pn_gamma'], 'L1_ffn_pn_beta': _L1_ffn_in['pn_beta'], 'L1_ffn_d1_w': _L1_ffn_in['d1_w'], 'L1_ffn_d1_b': _L1_ffn_in['d1_b'], 'L1_ffn_d2_w': _L1_ffn_in['d2_w'], 'L1_ffn_d2_b': _L1_ffn_in['d2_b'], 'L1_ffn_bc_w': _L1_ffn_in['bc_w'], 'L1_ffn_bc_b': _L1_ffn_in['bc_b'], 'L1_ffn_gate_w': _L1_ffn_in['gate_w'], 'L1_ffn_gate_b': _L1_ffn_in['gate_b'], 'L1_ffn_out_gamma': _L1_ffn_in['out_gamma'], 'L1_ffn_out_beta': _L1_ffn_in['out_beta']}
    _x0 = _d['L0_attn_x']
    _d['L0_attn_x'] = jax.random.normal(jax.random.fold_in(jax.random.key(seed), 1), (8, 512, 512), dtype=_x0.dtype)
    del _x0
    return _d

def reference(L0_attn_x, L0_attn_wq, L0_attn_wk, L0_attn_wv, L0_attn_wo, L0_ffn_gate_w, L0_ffn_gate_scale, L0_ffn_up_w, L0_ffn_up_scale, L0_ffn_down_w, L0_ffn_down_scale, L1_attn_wq, L1_attn_wk, L1_attn_wv, L1_attn_wo, L1_ffn_in_gamma, L1_ffn_in_beta, L1_ffn_agg_w, L1_ffn_agg_b, L1_ffn_pn_gamma, L1_ffn_pn_beta, L1_ffn_d1_w, L1_ffn_d1_b, L1_ffn_d2_w, L1_ffn_d2_b, L1_ffn_bc_w, L1_ffn_bc_b, L1_ffn_gate_w, L1_ffn_gate_b, L1_ffn_out_gamma, L1_ffn_out_beta):

    def _L0_attn_ref(x, wq, wk, wv, wo):
        import jax, jax.numpy as jnp
        import numpy as np
        B, S, D = (2, 1024, 512)
        H, HKV, DH = (16, 4, 128)
        CHUNK = 64
        GROUPS = H // HKV

        def _alibi_slopes(n_heads):
            i = jnp.arange(1, n_heads + 1, dtype=jnp.float32)
            return jnp.exp2(-8.0 * i / n_heads)

        def _rope(x):
            s, d = (x.shape[2], x.shape[3])
            inv_freq = 1.0 / 10000.0 ** (jnp.arange(0, d, 2, dtype=jnp.float32) / d)
            freqs = jnp.arange(s, dtype=jnp.float32)[:, None] * inv_freq[None, :]
            cos = jnp.concatenate([jnp.cos(freqs), jnp.cos(freqs)], axis=-1)
            sin = jnp.concatenate([jnp.sin(freqs), jnp.sin(freqs)], axis=-1)
            x1, x2 = (x[..., :d // 2], x[..., d // 2:])
            rot = jnp.concatenate([-x2, x1], axis=-1)
            return x * cos[None, None] + rot * sin[None, None]

        def _lightning_attn(q, k, v):
            b, h, s, dh = q.shape
            nc = s // CHUNK
            lam = _alibi_slopes(h)
            r = jnp.arange(CHUNK, dtype=jnp.float32)
            diff = r[:, None] - r[None, :]
            diag = jnp.where(diff >= 0, jnp.exp(-lam[:, None, None] * diff), 0.0)
            q_dec = jnp.exp(-lam[:, None] * (r + 1.0))
            k_dec = jnp.exp(-lam[:, None] * (CHUNK - 1.0 - r))
            blk = jnp.exp(-lam * CHUNK)
            qc = q.reshape(b, h, nc, CHUNK, dh).transpose(2, 0, 1, 3, 4)
            kc = k.reshape(b, h, nc, CHUNK, dh).transpose(2, 0, 1, 3, 4)
            vc = v.reshape(b, h, nc, CHUNK, dh).transpose(2, 0, 1, 3, 4)

            def step(kv, inp):
                qi, ki, vi = inp
                scores = jnp.einsum('bhid,bhjd->bhij', qi, ki) * diag[None]
                o_intra = jnp.einsum('bhij,bhje->bhie', scores, vi)
                o_inter = jnp.einsum('bhid,bhde->bhie', qi * q_dec[None, :, :, None], kv)
                kv = blk[None, :, None, None] * kv + jnp.einsum('bhjd,bhje->bhde', ki * k_dec[None, :, :, None], vi)
                return (kv, o_intra + o_inter)
            kv0 = jnp.zeros((b, h, dh, dh), q.dtype)
            _, o = jax.lax.scan(step, kv0, (qc, kc, vc))
            return o.transpose(1, 2, 0, 3, 4).reshape(b, h, s, dh)
        b, s, _ = x.shape
        q = jnp.einsum('bsd,ed->bse', x, wq).reshape(b, s, H, DH).transpose(0, 2, 1, 3)
        k = jnp.einsum('bsd,ed->bse', x, wk).reshape(b, s, HKV, DH).transpose(0, 2, 1, 3)
        v = jnp.einsum('bsd,ed->bse', x, wv).reshape(b, s, HKV, DH).transpose(0, 2, 1, 3)
        q = _rope(q)
        k = _rope(k)
        k = jnp.repeat(k, GROUPS, axis=1)
        v = jnp.repeat(v, GROUPS, axis=1)
        o = _lightning_attn(q, k, v)
        o = o.transpose(0, 2, 1, 3).reshape(b, s, H * DH)
        return jnp.einsum('bse,de->bsd', o, wo)

    def _L0_ffn_ref(hidden_state, gate_w, gate_scale, up_w, up_scale, down_w, down_scale):
        import jax, jax.numpy as jnp
        import numpy as np
        ZERO_POINT = 128.0

        def _dequant(wq, scale):
            return (wq.astype(jnp.float32) - ZERO_POINT) * scale[:, None]
        Wg = _dequant(gate_w, gate_scale)
        Wu = _dequant(up_w, up_scale)
        Wd = _dequant(down_w, down_scale)
        g = jnp.einsum('bsh,ih->bsi', hidden_state, Wg)
        u = jnp.einsum('bsh,ih->bsi', hidden_state, Wu)
        h = jax.nn.silu(g) * u
        return jnp.einsum('bsi,hi->bsh', h, Wd)

    def _L1_attn_ref(x, wq, wk, wv, wo):
        import jax, jax.numpy as jnp
        import numpy as np
        import math
        D = 512
        H = 32
        HKV = 8
        HD = D // H
        ROPE_BASE = 10000.0

        def _rope_cache(T, hd, base=ROPE_BASE):
            theta = 1.0 / base ** (jnp.arange(0, hd, 2, dtype=jnp.float32) / hd)
            t = jnp.arange(T, dtype=jnp.float32)
            freqs = t[:, None] * theta[None, :]
            return (jnp.cos(freqs), jnp.sin(freqs))

        def _apply_rope(x, cos, sin):
            B, Hh, T, hd = x.shape
            x_ = x.reshape(B, Hh, T, hd // 2, 2)
            x1, x2 = (x_[..., 0], x_[..., 1])
            c = cos[None, None, :, :]
            s = sin[None, None, :, :]
            rx1 = x1 * c - x2 * s
            rx2 = x1 * s + x2 * c
            return jnp.stack([rx1, rx2], axis=-1).reshape(B, Hh, T, hd)
        B, T, _ = x.shape
        q = (x @ wq.T).reshape(B, T, H, HD).transpose(0, 2, 1, 3)
        k = (x @ wk.T).reshape(B, T, HKV, HD).transpose(0, 2, 1, 3)
        v = (x @ wv.T).reshape(B, T, HKV, HD).transpose(0, 2, 1, 3)
        cos, sin = _rope_cache(T, HD)
        q = _apply_rope(q, cos, sin)
        k = _apply_rope(k, cos, sin)
        rep = H // HKV
        k = jnp.repeat(k, rep, axis=1)
        v = jnp.repeat(v, rep, axis=1)
        scores = jnp.einsum('bhtd,bhsd->bhts', q, k) / math.sqrt(HD)
        mask = jnp.triu(jnp.full((T, T), -jnp.inf, dtype=scores.dtype), k=1)
        scores = scores + mask[None, None, :, :]
        attn = jax.nn.softmax(scores, axis=-1)
        y = jnp.einsum('bhts,bhsd->bhtd', attn, v)
        y = y.transpose(0, 2, 1, 3).reshape(B, T, D)
        return y @ wo.T

    def _L1_ffn_ref(x, in_gamma, in_beta, agg_w, agg_b, pn_gamma, pn_beta, d1_w, d1_b, d2_w, d2_b, bc_w, bc_b, gate_w, gate_b, out_gamma, out_beta):
        import jax, jax.numpy as jnp
        import numpy as np
        EPS = 1e-06
        K_STEPS = 4
        USE_GATING = True

        def layer_norm(x, gamma, beta):
            mu = jnp.mean(x, axis=-1, keepdims=True)
            var = jnp.mean(jnp.square(x - mu), axis=-1, keepdims=True)
            return (x - mu) * jax.lax.rsqrt(var + EPS) * gamma + beta
        x_norm = layer_norm(x, in_gamma, in_beta)
        thought = x_norm[:, -1, :] @ agg_w + agg_b
        for _ in range(K_STEPS):
            t = layer_norm(thought, pn_gamma, pn_beta)
            t = jax.nn.gelu(t @ d1_w + d1_b, approximate=False)
            thought = thought + (t @ d2_w + d2_b)
        broadcast = (thought @ bc_w + bc_b)[:, None, :]
        if USE_GATING:
            gate = jax.nn.sigmoid(x @ gate_w + gate_b)
            out = x + gate * broadcast
        else:
            out = x + broadcast
        return layer_norm(out, out_gamma, out_beta)
    x = L0_attn_x
    x = x + _layernorm(_L0_attn_ref(_layernorm(x, axis=-1), L0_attn_wq, L0_attn_wk, L0_attn_wv, L0_attn_wo), axis=-1)
    x = x + _layernorm(_L0_ffn_ref(_layernorm(x, axis=-1), L0_ffn_gate_w, L0_ffn_gate_scale, L0_ffn_up_w, L0_ffn_up_scale, L0_ffn_down_w, L0_ffn_down_scale), axis=-1)
    x = x + _layernorm(_L1_attn_ref(_layernorm(x, axis=-1), L1_attn_wq, L1_attn_wk, L1_attn_wv, L1_attn_wo), axis=-1)
    x = x + _layernorm(_L1_ffn_ref(_layernorm(x, axis=-1), L1_ffn_in_gamma, L1_ffn_in_beta, L1_ffn_agg_w, L1_ffn_agg_b, L1_ffn_pn_gamma, L1_ffn_pn_beta, L1_ffn_d1_w, L1_ffn_d1_b, L1_ffn_d2_w, L1_ffn_d2_b, L1_ffn_bc_w, L1_ffn_bc_b, L1_ffn_gate_w, L1_ffn_gate_b, L1_ffn_out_gamma, L1_ffn_out_beta), axis=-1)
    return x

_drawn_inputs = setup_inputs


def setup_inputs(seed=0):
    import zlib

    import numpy as np

    out = dict(_drawn_inputs(seed))
    spreads = {'L1_ffn_in_gamma': (1.0, 0.6),
     'L1_ffn_in_beta': (0.0, 0.8),
     'L1_ffn_agg_b': (0.0, 0.49),
     'L1_ffn_pn_gamma': (1.0, 0.6),
     'L1_ffn_pn_beta': (0.0, 0.8),
     'L1_ffn_d1_b': (0.0, 0.459),
     'L1_ffn_d2_b': (0.0, 0.1),
     'L1_ffn_bc_b': (0.0, 0.471),
     'L1_ffn_gate_b': (0.0, 0.8),
     'L1_ffn_out_gamma': (1.0, 0.2),
     'L1_ffn_out_beta': (0.0, 0.1)}
    factors = {'L1_ffn_gate_w': 3.042}
    for name, (base, spread) in spreads.items():
        noise = np.random.default_rng([zlib.crc32(name.encode()), seed]).standard_normal(out[name].shape)
        drawn = base * np.exp(spread * noise) if base else spread * noise
        out[name] = jnp.asarray(drawn.astype(out[name].dtype))
    for name, factor in factors.items():
        out[name] = (out[name] * factor).astype(out[name].dtype)
    return out
```

```python
from contextlib import ExitStack

import concourse.bass as bass
from concourse import mybir

ALU = mybir.AluOpType
ACT = mybir.ActivationFunctionType
F32 = mybir.dt.float32
F32R = mybir.dt.float32r
BF16 = mybir.dt.bfloat16
I32 = mybir.dt.int32
AX_X = mybir.AxisListType.X

P = 128
S = 512
D = 512
KD = D // P
NT = S // P
H0, KV0, DH0 = 16, 4, 128
HG = H0 // KV0
I0 = 2048
NQ = 4
IC = I0 // NQ // P
H1, KV1, HD1 = 32, 8, 16
LN_EPS = 1e-5
ZERO_POINT = 128.0
BLOCKS = [(i, j) for i in range(NT) for j in range(i + 1)]
NBLK = len(BLOCKS)
LAG = 3
HEADS1 = [(q, n) for q in range(2) for n in range(2)]
SINGLE, DOUBLE = [[h] for h in HEADS1], [HEADS1[:2], HEADS1[2:]]
S1_BANKS = [(i, hs) for i, sets in ((0, DOUBLE), (1, DOUBLE), (2, SINGLE), (3, SINGLE)) for hs in sets]
S2_BANKS = [(j, hs) for j, sets in ((0, SINGLE), (1, SINGLE), (2, DOUBLE), (3, DOUBLE)) for hs in sets]
NS = len(S1_BANKS)
K_STEPS = 4
EPS_FFN = 1e-6
R = 32
ROW_M = 48
MASKED = -1e30


class Signal:

    def __init__(self, semaphore, stages, credit=0):
        self.sem, self.credit, self.offset, self.per = semaphore, credit, {}, {}
        at = 0
        for name, per, inner in stages:
            self.offset[name], self.per[name] = at, per
            at += per * inner
        self.total = at

    def at(self, stage, b, g, k):
        value = self.offset[stage] + k + self.credit
        if self.total:
            value = b * self.total + value
        return value if g is None else g * self.per[stage] + value


W_COLS = 6144
PIECE = (0, 4096)
CHUNK = 1024
CHUNKS = ({"a": 3, "b": 4, "c": 3, "d": 2}, {"a": 2, "b": 2, "c": 2})
SPLIT_AT = {0: (1, 0), 1: (1, 1), 4: (0, 0), 5: (0, 1), 6: (0, 2), 7: (0, 3)}
HANDOVER = [("post", 0), ("post", 1), ("pre", 0), ("post", 2), ("pre", 1), ("post", 3), ("pre", 2), ("pre", 3)]
assert len(HANDOVER) == 2 * NT


def build(nc, x, w_a, w_b, gate_scale, up_scale, down_scale,
          w_c, rope1_tables, causal, identity_b,
          w_gate, gate_b, agg_w, d1_w, d2_w, bc_w, in_gamma, in_beta, agg_b, pn_gamma, pn_beta, d1_b, d2_b,
          bc_b, out_gamma, out_beta, row_sum,
          rope0_cos, rope0_sin, decay, identity, out):
    NB = x.shape[0]
    x3_dram = nc.dram_tensor("x3_dram", [NB, S, D], F32, kind="Internal").ap()
    gate_dram = nc.dram_tensor("gate_dram", [NB, S, D], F32, kind="Internal").ap()
    bc_dram = nc.dram_tensor("bc_dram", [NB, D], F32, kind="Internal").ap()
    NL = 7 * NT

    with ExitStack() as ctx:
        def sb(name, shape, dt=F32, c=ctx):
            return c.enter_context(nc.sbuf_tensor(name, shape, dt))

        def sem(name):
            return ctx.enter_context(nc.semaphore(name))

        def signal(name, stages, credit=0):
            return Signal(sem(name), stages, credit)

        X = sb("X", [P, NT, D])
        xn = sb("xn", [P, 2, D])
        XnT = [sb(f"XnT_{n}", [P, KD, S], F32R) for n in ("hi", "lo")]
        w_raw = sb("w_raw", [P, W_COLS])
        W = [sb(f"w_{n}", [P, W_COLS], F32R) for n in ("hi", "lo")]
        y_acc = sb("y_acc", [P, NT, D])
        ident = sb("ident", [P, P])
        eps, minus_half = sb("eps", [P, 1]), sb("minus_half", [P, 1])
        stats, moments = sb("stats", [P, NL, 6]), sb("moments", [P, NL, 2])
        var_eps, rstd = sb("var_eps", [P, NL]), sb("rstd", [P, NL])

        def ring(name):
            return [ctx.enter_context(nc.psum_tensor(f"{name}{n}", [P, 512], F32)) for n in range(2)]

        proj_ps, score_ps, o_ps, y_ps = ring("proj_ps"), ring("score_ps"), ring("o_ps"), ring("y_ps")

        PROJ_A = 4 + HG
        in_proj = [("front_a", NT, 1), ("a", PROJ_A, KV0), ("front_b", NT, 1), ("b", IC, NQ),
                   ("front_c", NT, 1), ("qkv", 2 * NT, 1), ("s2", NS * KV1, 1), ("front_y", NT, 1),
                   ("front_d", NT, 1)]
        in_score = [("a", NBLK, KV0), ("b", IC, NQ), ("pack", 6 * NT, 1), ("s1", NS * KV1, 1)]
        in_y = [("a", NT, KV0), ("b", NT, NQ), ("c", NT, 1), ("d", NT, 1)]
        proj, proj_free = signal("s_proj", in_proj), signal("s_proj_free", in_proj, 2)
        score = signal("s_score", in_score)
        o_free = signal("s_o_free", [("a", NT, KV0)], 2)
        y, y_free = signal("s_y", in_y, 1), signal("s_y_free", in_y, 2)

        in_ln = [("ln", NL, 1)]
        ln_stats, ln_moments, ln_var, ln_rstd, ln_out = (signal(n, in_ln) for n in (
            "s_ln_stats", "s_ln_moments", "s_ln_var", "s_ln_rstd", "s_ln_out"))
        front_hi = signal("s_front_hi", [(n, NT, 1) for n in ("a", "b", "c", "y", "d")])
        resid = signal("s_resid", [(n, NT, 1) for n in ("a", "b", "c")])
        cleared = signal("s_cleared", [("a", 1, 1), ("b", 1, 1)])

        inner = {"a": KV0, "b": NQ, "c": 1, "d": 1}
        in_w = [[(s_, n_, inner[s_]) for s_, n_ in CHUNKS[n].items()] for n in range(2)]
        w_in = [signal(f"s_w_in{n}", [(s_, 16, m_) for s_, _, m_ in in_w[n]]) for n in range(2)]
        w_hi = [signal(f"s_w_hi{n}", in_w[n]) for n in range(2)]
        w_lo = [signal(f"s_w_lo{n}", in_w[n], 1) for n in range(2)]
        s_pool_const, s_ident = sem("s_pool_const"), sem("s_ident")
        s_carry = sem("s_carry")
        x_in = signal("s_x_in", [("x", 16, 1)])
        stored = signal("s_stored", [("x", 32, 1)], 32)
        gate_done = signal("s_gate", [("d", NT, 1)])

        A = ExitStack()
        cosT, sinT = sb("cosT", [P, S], c=A), sb("sinT", [P, S], c=A)
        dec = sb("dec", [P, HG, NT, P], c=A)
        qT = [sb(f"qT_{n}", [P, HG, S], F32R, A) for n in ("hi", "lo")]
        kT = [sb(f"kT_{n}", [P, S], F32R, A) for n in ("hi", "lo")]
        vT = sb("vT", [P, S], c=A)
        v = [sb(f"v_{n}", [P, NT, P], F32R, A) for n in ("hi", "lo")]
        swapped, sines = sb("swapped", [P, 2, S], c=A), sb("sines", [P, 2, S], c=A)
        roped = sb("roped", [P, 3, S], c=A)
        pf = sb("pf", [P, 2, 512], c=A)
        pT = [sb(f"pT_{n}", [P, 4, 512], F32R, A) for n in ("hi", "lo")]
        oT = [sb(f"oT_{n}", [P, HG, S], F32R, A) for n in ("hi", "lo")]
        A.close()
        NU = 1 + HG
        in_rope = [("a", NU, KV0)]
        tables_in = signal("s_tables_in", [("a", 32, 1)])
        decay_in = signal("s_decay_in", [("a", 16, KV0)])
        swap_done = signal("s_swap", [("a", 2 * NU, KV0)])
        sin_done, rope_hi = signal("s_sin", in_rope, 1), signal("s_rope_hi", in_rope)
        rope_sum, rope_lo = signal("s_rope_sum", in_rope, 1), signal("s_rope_lo", in_rope, 1)
        vT_done = signal("s_vT", [("a", 1, KV0)])
        v_hi, v_lo = signal("s_v_hi", [("a", 2, KV0)]), signal("s_v_lo", [("a", 2, KV0)])
        in_blk = [("a", NBLK, KV0)]
        p_f, p_hi = signal("s_p_f", in_blk, 2), signal("s_p_hi", in_blk)
        p_lo, pv_done = signal("s_p_lo", in_blk, 2), signal("s_pv", in_blk, 4)
        o_hi, o_lo = signal("s_o_hi", [("a", NT, KV0)]), o_free

        B = ExitStack()
        gsc, usc = sb("gsc", [P, I0 // P], c=B), sb("usc", [P, I0 // P], c=B)
        dsc = sb("dsc", [P, D], c=B)
        silu, hf = sb("silu", [P, 2, S], c=B), sb("hf", [P, 2, S], c=B)
        hT = [sb(f"hT_{n}", [P, IC, S], F32R, B) for n in ("hi", "lo")]
        B.close()
        scales_in = signal("s_scales_in", [("b", 48, 1)])
        in_h = [("b", IC, NQ)]
        h_f = signal("s_h_f", in_h, 2)
        h_hi, h_lo = signal("s_h_hi", in_h), signal("s_h_lo", in_h, 2)
        y_scaled = signal("s_y_scaled", [("b", NT, 1)])

        C = ExitStack()
        rope1 = sb("rope1", [P, 4, NT, HD1], c=C)
        mask = sb("mask", [P, P], BF16, C)
        ident_b = sb("ident_b", [P, P], BF16, C)
        ra, rb = sb("ra", [P, (H1 + KV1) * HD1], c=C), sb("rb", [P, (H1 + KV1) * HD1], c=C)
        q_pack = sb("q_pack", [P, H1, 64], F32R, C)
        k_pack = sb("k_pack", [P, KV1, 2, 64], F32R, C)
        QT = sb("QT", [P, H1 // 2, S], F32R, C)
        KT = sb("KT", [P, KV1, S], F32R, C)
        V1 = sb("V1", [P, NT, KV1, 32], c=C)
        row_max = sb("row_max", [P, KV1, NT, 2, 2], c=C)
        maxT = sb("maxT", [4, 2, S], F32R, C)
        probs = [sb(f"probs{j}", [P, 4, S - j * P], c=C) for j in range(NT)]
        yT = xn
        rden = sb("rden", [P, 2, NT * 4], c=C)
        gate_bias = sb("gate_bias", [P, D], c=C)
        C.close()
        NR, NQC = H1 * HD1, KV1 * HD1
        consts1_in = signal("s_consts1_in", [("c", 64, 1)])
        pads = signal("s_pads", [("c", 5, 1)])
        in_t = [("c", 2 * NT, 1)]
        rot_sum, rot_lo = signal("s_rot_sum", in_t, 1), signal("s_rot_lo", in_t, 1)
        rot_hi = signal("s_rot_hi", [("c", 4 * NT, 1)])
        rot_k = signal("s_rot_k", [("c", NT, 1)])
        moved = [signal(f"s_moved{n}", [("c", 3 * NT, 1)], 1) for n in range(2)]
        s_max = signal("s_max", [("c", NS * KV1, 1)], 2)
        in_g = [("c", KV1, 1)]
        max_rows, maxT_done = signal("s_max_rows", in_g), signal("s_maxT", in_g)
        m_in = signal("s_m_in", [("c", 32 * KV1, 1)], 16)
        masked, pv1 = signal("s_masked", [("c", NT * KV1, 1)]), signal("s_pv1", [("c", NT * KV1, 1)], 4)
        yT_done, y_back = signal("s_yT", in_g, 2), signal("s_y_back", in_g)
        den_done, y1_done = signal("s_den", in_g), signal("s_y1", in_g, 2)

        Dx = ExitStack()
        d1w, d2w = sb("d1w", [P, KD, I0], c=Dx), sb("d2w", [P, I0 // P, D], c=Dx)
        aggw, bcw = (w_raw[:, n * KD * D:(n + 1) * KD * D].rearrange("p (k n) -> p k n", k=KD) for n in range(2))
        row_consts = sb("row_consts", [R, 7, D], c=Dx)
        thought, rows = sb("thought", [R, D], c=Dx), sb("rows", [R, D], c=Dx)
        bias1, gam, bet = sb("bias1", [P, D], c=Dx), sb("gam", [P, D], c=Dx), sb("bet", [P, D], c=Dx)
        rowsT, hiddenT = sb("rowsT", [P, KD, R], c=Dx), sb("hiddenT", [P, KD, P], c=Dx)
        summing = sb("summing", [P, R], c=Dx)
        eps_ffn = sb("eps_ffn", [P, 1], c=Dx)
        bcast = sb("bcast", [P, 2, D], c=Dx)
        Dx.close()
        Z, G = y_acc, w_raw[:, 2 * KD * D:3 * KD * D].rearrange("p (t d) -> p t d", t=NT)
        hidden, partial = xn[:, 0, :], xn[:, 1, :]
        row_in, d_in = sem("s_row_in"), sem("s_d_in")
        in_row = [("pre", 10, 1), ("step", 11, K_STEPS), ("post", 2, 1)]
        row = signal("s_row", in_row)
        row_mm = signal("s_row_mm", [("pre", 2, 1), ("step", 5, K_STEPS), ("post", 2, 1)])
        row_var, row_rstd = (signal(n, [("pre", 2, 1), ("step", 1, K_STEPS)]) for n in ("s_row_var", "s_row_rstd"))
        gelu_done = signal("s_gelu", [("step", 1, K_STEPS)])
        s_rows_clear, s_bc_out, s_eps2 = sem("s_rows_clear"), sem("s_bc_out"), sem("s_eps2")
        in_o = [("o", NT, 1)]
        x3_in = [signal(f"s_x3_in{t}", [("o", 32, 1)]) for t in range(NT)]
        out_stored = [signal(f"s_out_stored{t}", [("o", 16, 1)], 16) for t in range(NT)]
        bc_in = signal("s_bc_in", [("o", 16, 1)])
        fin_step = signal("s_fin_step", [("o", 14 * NT, 1)])
        fin_var, fin_rstd = signal("s_fin_var", [("o", 3 * NT, 1)]), signal("s_fin_rstd", [("o", 3 * NT, 1)])

        block = ctx.enter_context(nc.Block())

        def wk(t, c):
            return t[:, c * P:(c + 1) * P]

        def wv(t, c):
            return t[:, (KD + c) * P:(KD + c + 1) * P]

        def wq(t, c, h):
            at = 2 * KD * P + c * HG * P + h * P
            return t[:, at:at + P]

        def wo(t, h):
            return t[:, PIECE[1] + h * D:PIECE[1] + (h + 1) * D]

        def wup(t, c, m):
            return t[:, c * 512 + m * P:c * 512 + (m + 1) * P]

        def wgate(t, c, m):
            return wup(t, KD + c, m)

        def chunk(t, n, c):
            return t[:, PIECE[n] + c * CHUNK:PIECE[n] + (c + 1) * CHUNK]

        def wkv1(t, c):
            return t[:, c * 2 * NQC:(c + 1) * 2 * NQC]

        def wq1(t, c):
            return t[:, KD * 2 * NQC + c * NR:KD * 2 * NQC + (c + 1) * NR]

        ROW_INS = 16 * 17
        W_A, W_B = (3072, 5120), (4096, 6144)
        S2_END = [sum(jj <= j for jj, _ in S2_BANKS) for j in range(NT)]
        LAST = [max(n for n, (i, j) in enumerate(BLOCKS) if i == q) for q in range(NT)]
        WO_AFTER = {LAST[0] + 2: [0], LAST[1] + 2: [1], LAST[3]: [2, 3]}
        WO_AFTER_BLOCK = {t: m + 1 for m, ts in WO_AFTER.items() for t in ts}

        @block.sync
        def _(sp):
            sp.dma_start(ident[:, :], identity).then_inc(s_ident, 16)
            sp.sem_inc(stored.sem, 32)
            sp.sem_inc(m_in.sem, 16)
            with sp.Fori(0, NB) as b:
                def load(n, stage, g, src, ends, dt=F32):
                    start, lo, hi = PIECE[n], (0, ends[0])[n], ends[n]
                    step = src if g is None else src[bass.ds(g, 1), :, :]
                    sp.wait_ge(w_lo[n].sem, w_lo[n].at(stage, b, g, 0))
                    sp.dma_start(w_raw[:, start:start + hi - lo].bitcast(dt),
                                 step[:, :, lo:hi].rearrange("a p n -> (a p) n"))\
                        .then_inc(w_in[n].sem, 16)

                load(0, "a", 0, w_a, W_A)
                sp.wait_ge(stored.sem, stored.at("x", b, None, 0))
                sp.dma_start(X[:, :, :], x[bass.ds(b, 1), :, :].rearrange("a (t p) d -> p (a t) d", p=P))\
                    .then_inc(x_in.sem, 16)
                sp.wait_ge(y_free.sem, y_free.at("a", b, None, 0))
                sp.dma_start(cosT[:, :], rope0_cos).then_inc(tables_in.sem, 16)
                sp.dma_start(sinT[:, :], rope0_sin).then_inc(tables_in.sem, 16)

                def load_decay(g):
                    sp.wait_ge(p_f.sem, p_f.at("a", b, g, 0))
                    sp.dma_start(dec[:, :, :, :].rearrange("p h t i -> p (h t i)"),
                                 decay[bass.ds(g, 1), :, :].rearrange("a p n -> (a p) n"))\
                        .then_inc(decay_in.sem, 16)

                with sp.Fori(0, KV0 - 1) as g:
                    load(1, "a", g, w_a, W_A)
                    load_decay(g)
                    load(0, "a", g + 1, w_a, W_A)
                load(1, "a", KV0 - 1, w_a, W_A)
                load_decay(KV0 - 1)
                load(0, "b", 0, w_b, W_B, I32)
                sp.wait_ge(resid.sem, resid.at("a", b, None, NT))
                sp.dma_start(gsc[:, :], gate_scale).then_inc(scales_in.sem, 16)
                sp.dma_start(usc[:, :], up_scale).then_inc(scales_in.sem, 16)
                sp.dma_start(dsc[:, :], down_scale.partition_broadcast(P)).then_inc(scales_in.sem, 16)
                with sp.Fori(0, NQ - 1) as g:
                    load(1, "b", g, w_b, W_B, I32)
                    load(0, "b", g + 1, w_b, W_B, I32)
                load(1, "b", NQ - 1, w_b, W_B, I32)
                load(0, "c", None, w_c, W_A)
                load(1, "c", None, w_c, W_A)
                sp.wait_ge(resid.sem, resid.at("b", b, None, NT))
                sp.dma_start(rope1[:, :, :, :].rearrange("p a t d -> p (a t d)"), rope1_tables).then_inc(consts1_in.sem, 16)
                sp.dma_start(mask[:, :], causal).then_inc(consts1_in.sem, 16)
                sp.dma_start(ident_b[:, :], identity_b).then_inc(consts1_in.sem, 16)
                sp.dma_start(gate_bias[:, :], gate_b.partition_broadcast(P)).then_inc(consts1_in.sem, 16)
                sp.wait_ge(w_lo[0].sem, w_lo[0].at("d", b, None, 0))
                sp.dma_start(w_raw[:, 0:KD * D], w_gate).then_inc(w_in[0].sem, 16)
                for g in range(KV1):
                    sp.wait_ge(maxT_done.sem, maxT_done.at("c", b, None, g + 1))
                    for q in range(2):
                        sp.dma_start(QT[64 * q + ROW_M:64 * q + ROW_M + 1, 2 * g:2 * g + 2, :].bitcast(F32),
                                     maxT[2 * q:2 * q + 2, g % 2, :].bitcast(F32)).then_inc(m_in.sem, 16)
                sp.wait_ge(resid.sem, resid.at("c", b, None, NT))
                sp.dma_start(x3_dram[bass.ds(b, 1), :, :].rearrange("a (t p) d -> p (a t) d", p=P), X[:, :, :])\
                    .then_inc(stored.sem, 16)
                sp.wait_ge(gate_done.sem, gate_done.at("d", b, None, NT))
                sp.dma_start(gate_dram[bass.ds(b, 1), :, :].rearrange("a (t p) d -> p (a t) d", p=P), y_acc[:, :, :])\
                    .then_inc(stored.sem, 16)
            sp.wait_ge(stored.sem, 32 * (NB + 1))

            sp.wait_ge(s_rows_clear, 1)
            sp.dma_start(rows[0:NB, :], x3_dram[:, S - 1, :]).then_inc(row_in, 16)
            sp.dma_start(aggw, agg_w).then_inc(row_in, 16)
            for n, c in enumerate((in_gamma, in_beta, agg_b, pn_gamma, pn_beta, d2_b, bc_b)):
                sp.dma_start(row_consts[:, n, :], c.partition_broadcast(R)).then_inc(row_in, 16)
            for n in range(4):
                sp.dma_start(bias1[32 * n:32 * n + 32, :], d1_b[n * D:(n + 1) * D].partition_broadcast(32)).then_inc(row_in, 16)
            sp.dma_start(summing[:, :], row_sum).then_inc(row_in, 16)
            sp.dma_start(d1w[:, :, :], d1_w).then_inc(row_in, 16)
            sp.dma_start(d2w[:, :, :], d2_w).then_inc(row_in, 16)
            sp.dma_start(bcw, bc_w).then_inc(row_in, 16)
            sp.dma_start(gam[:, :], out_gamma.partition_broadcast(P)).then_inc(d_in, 16)
            sp.dma_start(bet[:, :], out_beta.partition_broadcast(P)).then_inc(d_in, 16)
            sp.wait_ge(row.sem, row.at("post", 0, None, 2))
            sp.dma_start(bc_dram, rows[0:NB, :]).then_inc(s_bc_out, 16)
            sp.wait_ge(s_bc_out, 16)
            with sp.Fori(0, NB) as b:
                sp.wait_ge(out_stored[NT - 1].sem, out_stored[NT - 1].at("o", b, None, 0))
                sp.dma_start(bcast[:, 0, :], bc_dram[bass.ds(b, 1), :].rearrange("a d -> (a d)").partition_broadcast(P))\
                    .then_inc(bc_in.sem, 16)
                for t in range(NT):
                    sp.wait_ge(out_stored[t].sem, out_stored[t].at("o", b, None, 0))
                    for dst, src in ((X, x3_dram), (G, gate_dram)):
                        sp.dma_start(dst[:, t, :], src[bass.ds(b, 1), t * P:(t + 1) * P, :].rearrange("a p d -> p (a d)"))\
                            .then_inc(x3_in[t].sem, 16)
            for t in range(NT):
                sp.wait_ge(out_stored[t].sem, 16 * (NB + 1))

        def move_pack(copy, t, u):
            src = score_ps[u % 2][:, :].rearrange("p (n i) -> p n i", i=P)
            dst = QT[:, 4 * u:4 * u + 4, t * P:(t + 1) * P] if u < 4 else KT[:, 4 * (u - 4):4 * (u - 3), t * P:(t + 1) * P]
            return copy(dst, src)

        @block.gpsimd
        def _(pool):
            pool.memset(eps[:, :], LN_EPS).then_inc(s_pool_const, 1)
            pool.memset(minus_half[:, :], -0.5).then_inc(s_pool_const, 1)
            pool.wait_ge(s_pool_const, 2)
            pool.sem_inc(sin_done.sem, 1)

            def rstds(b, n):
                pool.wait_ge(ln_moments.sem, ln_moments.at("ln", b, None, n + 1))
                pool.tensor_tensor(var_eps[:, n:n + 1], moments[:, n, 1:2], eps[:, :], ALU.add)\
                    .then_inc(ln_var.sem, 1)
                pool.wait_ge(ln_var.sem, ln_var.at("ln", b, None, n + 1))
                pool.tensor_tensor(rstd[:, n:n + 1], var_eps[:, n:n + 1], minus_half[:, :], ALU.pow)\
                    .then_inc(ln_rstd.sem, 1)

            with pool.Fori(0, NB) as b:
                for t in range(NT):
                    rstds(b, t)
                pool.wait_ge(stored.sem, stored.at("x", b, None, 0))
                pool.sem_inc(s_carry, 1)
                pool.memset(y_acc[:, :, :], 0.0).then_inc(cleared.sem, 1)
                def a_step(g, last):
                    pool.wait_ge(tables_in.sem, tables_in.at("a", b, None, 32))
                    for u in range(NU):
                        pool.wait_ge(rope_sum.sem, rope_sum.at("a", b, g, max(u - 1, 0)))
                        pool.wait_ge(swap_done.sem, swap_done.at("a", b, g, 2 * u + 2))
                        pool.tensor_tensor(sines[:, u % 2, :], swapped[:, u % 2, :], sinT[:, :], ALU.mult)\
                            .then_inc(sin_done.sem, 1)
                    for n in range(NBLK):
                        pool.wait_ge(p_hi.sem, p_hi.at("a", b, g, n + 1))
                        pool.tensor_tensor(pT[1][:, n % 4, :], pf[:, n % 2, :], pT[0][:, n % 4, :].bitcast(F32),
                                           ALU.subtract).then_inc(p_lo.sem, 1)
                        if last and n == WO_AFTER_BLOCK[0] + LAG:
                            rstds(b, NT)
                        if last and n == WO_AFTER_BLOCK[1] + LAG:
                            rstds(b, NT + 1)

                with pool.Fori(0, KV0 - 1) as g:
                    a_step(g, False)
                a_step(KV0 - 1, True)
                for n in range(2, 2 * NT):
                    rstds(b, NT + n)
                pool.wait_ge(resid.sem, resid.at("a", b, None, NT))
                pool.sem_inc(s_carry, 1)
                pool.memset(y_acc[:, :, :], 0.0).then_inc(cleared.sem, 1)
                with pool.Fori(0, NQ) as g:
                    for m in range(IC):
                        pool.wait_ge(h_hi.sem, h_hi.at("b", b, g, m + 1))
                        pool.tensor_tensor(hT[1][:, m, :], hf[:, m % 2, :], hT[0][:, m, :].bitcast(F32),
                                           ALU.subtract).then_inc(h_lo.sem, 1)
                for t in range(2 * NT):
                    rstds(b, 3 * NT + t)
                pool.wait_ge(resid.sem, resid.at("b", b, None, 1))
                pool.sem_inc(s_carry, 1)
                pool.memset(q_pack[:, :, ROW_M:64].bitcast(F32), 0.0).then_inc(pads.sem, 1)
                pool.memset(k_pack[:, :, :, ROW_M:ROW_M + 1].bitcast(F32), -1.0).then_inc(pads.sem, 1)
                pool.memset(k_pack[:, :, :, ROW_M + 1:64].bitcast(F32), 0.0).then_inc(pads.sem, 1)
                pool.memset(V1[:, :, :, HD1:HD1 + 1], 1.0).then_inc(pads.sem, 1)
                pool.memset(V1[:, :, :, HD1 + 1:32], 0.0).then_inc(pads.sem, 1)
                for g in range(KV1):
                    for j in range(NT):
                        pool.wait_ge(proj_free.sem, proj_free.at("s2", b, None, g * NS + S2_END[j]))
                        pool.sem_inc(s_carry, 1)
                        pool.affine_select(out=probs[j][:, :, 0:P], in_=probs[j][:, :, 0:P], compare_op=ALU.is_ge,
                                           fill=0.0, base=0, pattern=[[0, 4], [1, P]], channel_multiplier=-1)\
                            .then_inc(masked.sem, 1)
                for t in range(2 * NT):
                    rstds(b, 5 * NT + t)

            def row_rstds(stage, g, k, eps_):
                pool.wait_ge(row.sem, row.at(stage, 0, g, 3 * k + 2))
                pool.tensor_tensor(var_eps[0:R, 0:1], moments[0:R, 0, 1:2], eps_[0:R, :], ALU.add).then_inc(row_var.sem, 1)
                pool.wait_ge(row_var.sem, row_var.at(stage, 0, g, k + 1))
                pool.tensor_tensor(rstd[0:R, 0:1], var_eps[0:R, 0:1], minus_half[0:R, :], ALU.pow).then_inc(row_rstd.sem, 1)

            pool.wait_ge(stored.sem, 32 * (NB + 1))
            pool.memset(eps_ffn[:, :], EPS_FFN).then_inc(s_eps2, 1)
            pool.memset(rows[:, :], 0.0).then_inc(s_rows_clear, 1)
            pool.wait_ge(s_eps2, 1)
            row_rstds("pre", None, 0, eps)
            row_rstds("pre", None, 1, eps_ffn)
            with pool.Fori(0, K_STEPS) as g:
                row_rstds("step", g, 0, eps_ffn)
            with pool.Fori(0, NB) as b:
                for t in range(NT):
                    for k, (at, eps_) in enumerate(((2, eps), (7, eps_ffn), (12, eps))):
                        n = 3 * t + k
                        pool.wait_ge(fin_step.sem, fin_step.at("o", b, None, 14 * t + at))
                        pool.tensor_tensor(var_eps[:, n:n + 1], moments[:, n, 1:2], eps_[:, :], ALU.add).then_inc(fin_var.sem, 1)
                        pool.wait_ge(fin_var.sem, fin_var.at("o", b, None, n + 1))
                        pool.tensor_tensor(rstd[:, n:n + 1], var_eps[:, n:n + 1], minus_half[:, :], ALU.pow)\
                            .then_inc(fin_rstd.sem, 1)

        @block.scalar
        def _(act):
            def copy(out_, in_):
                return act.activation(out_, in_, ACT.Copy)

            def front(stage, b):
                for t in range(NT):
                    act.wait_ge(proj.sem, proj.at("front_" + stage, b, None, t + 1))
                    copy(XnT[0][:, :, t * P:(t + 1) * P],
                         proj_ps[t % 2][:, :].rearrange("p (k i) -> p k i", k=KD)).then_inc(front_hi.sem, 1)

            act.sem_inc(moved[0].sem, 1)
            for t in range(NT):
                act.sem_inc(out_stored[t].sem, 16)
            with act.Fori(0, NB) as b:
                def split(n, stage, g, c):
                    if c == 0:
                        act.wait_ge(w_in[n].sem, w_in[n].at(stage, b, g, 16))
                    src, bias = (chunk(w_raw, n, c).bitcast(I32), -ZERO_POINT) if stage == "b" else (chunk(w_raw, n, c), 0.0)
                    act.activation(chunk(W[0], n, c), src, ACT.Copy, bias=bias).then_inc(w_hi[n].sem, 1)

                for c in range(CHUNKS[0]["a"]):
                    split(0, "a", 0, c)
                front("a", b)

                def a_step(g, following):
                    def swap(u, use):
                        act.wait_ge(sin_done.sem, sin_done.at("a", b, g, max(u - 1, 0)))
                        act.wait_ge(proj.sem, proj.at("a", b, g, use + 1))
                        half = P // 2
                        ps = proj_ps[use % 2]
                        copy(swapped[0:half, u % 2, :], ps[half:P, :]).then_inc(swap_done.sem, 1)
                        copy(swapped[half:P, u % 2, :], ps[0:half, :]).then_inc(swap_done.sem, 1)

                    def rope_high(u):
                        act.wait_ge(rope_sum.sem, rope_sum.at("a", b, g, u + 1))
                        dst = kT[0][:, :] if u == 0 else qT[0][:, u - 1, :]
                        copy(dst, roped[:, u % 3, :]).then_inc(rope_hi.sem, 1)

                    swap(0, 0)
                    swap(1, 1)
                    rope_high(0)
                    swap(2, 2)
                    rope_high(1)
                    swap(3, 4)
                    rope_high(2)
                    swap(4, 5)
                    rope_high(3)
                    for n in range(2):
                        act.wait_ge(proj.sem, proj.at("a", b, g, 7 + n))
                        copy(v[0][:, 2 * n:2 * n + 2, :], proj_ps[n][:, 0:2 * P].rearrange("p (t e) -> p t e", t=2))\
                            .then_inc(v_hi.sem, 1)
                        if n == 0:
                            rope_high(4)
                    act.wait_ge(y.sem, y.at("a", b, g, 0))
                    for n in range(NBLK + LAG):
                        if n < NBLK:
                            act.wait_ge(pv_done.sem, pv_done.at("a", b, g, n - 3))
                            act.wait_ge(p_f.sem, p_f.at("a", b, g, n + 1))
                            copy(pT[0][:, n % 4, :], pf[:, n % 2, :]).then_inc(p_hi.sem, 1)
                            part, c = SPLIT_AT.get(n, (None, 0))
                            if part == 1:
                                split(1, "a", g, c)
                            elif part == 0 and c < CHUNKS[0][following[0]]:
                                split(0, *following, c)
                        if n - LAG in LAST:
                            i = LAST.index(n - LAG)
                            act.wait_ge(pv_done.sem, pv_done.at("a", b, g, n - LAG + 1))
                            copy(oT[0][:, :, i * P:(i + 1) * P], o_ps[i % 2][:, :].rearrange("p (h i) -> p h i", h=HG))\
                                .then_inc(o_hi.sem, 1)

                with act.Fori(0, KV0 - 1) as g:
                    a_step(g, ("a", g + 1))
                a_step(KV0 - 1, ("b", 0))
                front("b", b)

                def b_step(g, following):
                    act.wait_ge(scales_in.sem, scales_in.at("b", b, None, 48))
                    act.wait_ge(y.sem, y.at("b", b, g, 0))
                    for m in range(IC):
                        act.wait_ge(h_f.sem, h_f.at("b", b, g, m - 1))
                        act.wait_ge(proj.sem, proj.at("b", b, g, m + 1))
                        act.activation(silu[:, m % 2, :], proj_ps[m % 2][:, :], ACT.Silu,
                                       scale=gsc[:, bass.ds(g * IC + m, 1)]).then_inc(proj_free.sem, 1)
                        if m >= 1:
                            act.wait_ge(h_f.sem, h_f.at("b", b, g, m))
                            copy(hT[0][:, m - 1, :], hf[:, (m - 1) % 2, :]).then_inc(h_hi.sem, 1)
                        if m < CHUNKS[1]["b"]:
                            split(1, "b", g, m)
                    act.wait_ge(h_f.sem, h_f.at("b", b, g, IC))
                    copy(hT[0][:, IC - 1, :], hf[:, (IC - 1) % 2, :]).then_inc(h_hi.sem, 1)
                    for c in range(CHUNKS[0][following[0]]):
                        split(0, *following, c)

                with act.Fori(0, NQ - 1) as g:
                    b_step(g, ("b", g + 1))
                b_step(NQ - 1, ("c", None))
                front("c", b)

                def moves(t):
                    for u in (0, 2, 4):
                        act.wait_ge(score.sem, score.at("pack", b, None, 6 * t + u + 1))
                        move_pack(copy, t, u).then_inc(moved[0].sem, 1)

                for t in range(NT):
                    if t >= 1:
                        moves(t - 1)
                        act.wait_ge(score.sem, score.at("pack", b, None, 6 * t))
                    else:
                        act.wait_ge(pads.sem, pads.at("c", b, None, 5))
                    q_, k_ = ra[:, 0:NR].rearrange("p (h d) -> p h d", h=H1), ra[:, NR:].rearrange("p (h d) -> p h d", h=KV1)
                    act.wait_ge(rot_sum.sem, rot_sum.at("c", b, None, 2 * t + 1))
                    for n in range(2):
                        copy(q_pack[:, :, n * HD1:(n + 1) * HD1], q_).then_inc(rot_hi.sem, 1)
                    act.wait_ge(rot_sum.sem, rot_sum.at("c", b, None, 2 * t + 2))
                    for n in range(2):
                        copy(k_pack[:, :, :, 2 * n * HD1:(2 * n + 1) * HD1],
                             k_.unsqueeze(2).to_broadcast([P, KV1, 2, HD1])).then_inc(rot_hi.sem, 1)
                moves(NT - 1)
                act.wait_ge(y.sem, y.at("c", b, None, 0))
                for c in range(CHUNKS[1]["c"]):
                    split(1, "c", None, c)
                for c in range(CHUNKS[0]["d"]):
                    split(0, "d", None, c)
                for g in range(KV1):
                    for u, (j, heads) in enumerate(S2_BANKS):
                        n = g * NS + u
                        if u == 0 or S2_BANKS[u - 1][0] != j:
                            act.wait_ge(pv1.sem, pv1.at("c", b, None, (g - 1) * NT + j + 1))
                        act.wait_ge(proj.sem, proj.at("s2", b, None, n + 1))
                        h0, w = HEADS1.index(heads[0]), S - j * P
                        act.activation(probs[j][:, h0:h0 + len(heads), :],
                                       proj_ps[n % 2][:, 0:len(heads) * w].rearrange("p (h i) -> p h i", i=w), ACT.Exp)\
                            .then_inc(proj_free.sem, 1)
                front("y", b)
                front("d", b)
                for t in range(NT):
                    act.wait_ge(y_free.sem, y_free.at("d", b, None, t + 1))
                    act.activation(y_acc[:, t, :], y_acc[:, t, :], ACT.Sigmoid).then_inc(gate_done.sem, 1)

            with act.Fori(0, K_STEPS) as g:
                act.wait_ge(row.sem, row.at("step", 0, g, 7))
                act.activation(hidden, hidden, ACT.Gelu).then_inc(gelu_done.sem, 1)
            with act.Fori(0, NB) as b:
                for t in range(NT):
                    act.wait_ge(fin_step.sem, fin_step.at("o", b, None, 14 * t + 14))
                    act.dma_start(out[bass.ds(b, 1), t * P:(t + 1) * P, :].rearrange("a p d -> p (a d)"), Z[:, t, :])\
                        .then_inc(out_stored[t].sem, 16)

        @block.vector
        def _(dve):
            for free in (proj_free, o_free, y_free, rope_sum, p_f, h_f):
                dve.sem_inc(free.sem, free.credit)
            for n in range(2):
                dve.sem_inc(w_lo[n].sem, 1)
            dve.sem_inc(p_lo.sem, 2)
            dve.sem_inc(rope_lo.sem, 1)
            dve.sem_inc(h_lo.sem, 2)
            for free in (rot_sum, rot_lo, moved[1], s_max, yT_done, y1_done):
                dve.sem_inc(free.sem, free.credit)

            def measure(b, n, src):
                dve.bn_stats(stats[:, n, :], src).then_inc(ln_stats.sem, 1)
                dve.wait_ge(ln_stats.sem, ln_stats.at("ln", b, None, n + 1))
                dve.sem_inc(s_carry, 1)
                dve.bn_aggr(moments[:, n, :], stats[:, n, :]).then_inc(ln_moments.sem, 1)

            def norm(b, n, dst, src):
                dve.wait_ge(ln_rstd.sem, ln_rstd.at("ln", b, None, n + 1))
                dve.tensor_scalar(dst, src, moments[:, n, 0:1], rstd[:, n:n + 1], ALU.subtract, ALU.mult)\
                    .then_inc(ln_out.sem, 1)

            def low(dst, full, high):
                return dve.tensor_tensor(dst, full, high.bitcast(F32), ALU.subtract)

            def front_low(stage, b, t):
                dve.wait_ge(front_hi.sem, front_hi.at(stage, b, None, t + 1))
                low(XnT[1][:, :, t * P:(t + 1) * P], proj_ps[t % 2][:, :].rearrange("p (k i) -> p k i", k=KD),
                    XnT[0][:, :, t * P:(t + 1) * P]).then_inc(proj_free.sem, 1)

            def handover(stage, following, base, b, k):
                if k < 2 * NT:
                    which, t = HANDOVER[k]
                    if which == "pre":
                        dve.wait_ge(resid.sem, resid.at(stage, b, None, t + 1))
                    measure(b, base + k, y_acc[:, t, :] if which == "post" else X[:, t, :])
                if k >= 1:
                    which, t = HANDOVER[k - 1]
                    n = base + k - 1
                    if which == "post":
                        norm(b, n, y_acc[:, t, :], y_acc[:, t, :])
                        dve.wait_ge(ln_out.sem, ln_out.at("ln", b, None, n + 1))
                        dve.tensor_tensor(X[:, t, :], X[:, t, :], y_acc[:, t, :], ALU.add).then_inc(resid.sem, 1)
                    else:
                        if t >= 2:
                            front_low(following, b, t - 2)
                        norm(b, n, xn[:, t % 2, :], X[:, t, :])

            HANDOVER_AT = {0: (0,), 1: (1,), 2: (2, 3), 3: (4, 5, 6, 7, 8)}

            def split(n, stage, b, g, c):
                dve.wait_ge(w_hi[n].sem, w_hi[n].at(stage, b, g, c + 1))
                if stage == "b":
                    last = dve.scalar_tensor_tensor(chunk(W[1], n, c), chunk(w_raw, n, c).bitcast(I32), -ZERO_POINT,
                                                    chunk(W[0], n, c).bitcast(F32), ALU.add, ALU.subtract)
                else:
                    last = low(chunk(W[1], n, c), chunk(w_raw, n, c), chunk(W[0], n, c))
                last.then_inc(w_lo[n].sem, 1)

            with dve.Fori(0, NB) as b:
                for c in range(CHUNKS[0]["a"]):
                    split(0, "a", b, 0, c)
                dve.wait_ge(x_in.sem, x_in.at("x", b, None, 16))
                for t in range(NT):
                    measure(b, t, X[:, t, :])
                for t in range(NT):
                    if t >= 2:
                        front_low("a", b, t - 2)
                    norm(b, t, xn[:, t % 2, :], X[:, t, :])
                for t in (NT - 2, NT - 1):
                    front_low("a", b, t)

                def a_step(g, following):
                    dve.wait_ge(tables_in.sem, tables_in.at("a", b, None, 32))

                    def cosine(u, use):
                        dve.wait_ge(rope_lo.sem, rope_lo.at("a", b, g, max(u - 2, 0)))
                        dve.wait_ge(swap_done.sem, swap_done.at("a", b, g, 2 * u + 2))
                        dve.tensor_tensor(roped[:, u % 3, :], proj_ps[use % 2][:, :], cosT[:, :], ALU.mult)\
                            .then_inc(proj_free.sem, 1)

                    def rotate(u, use):
                        dve.wait_ge(proj_free.sem, proj_free.at("a", b, g, use + 1))
                        dve.wait_ge(sin_done.sem, sin_done.at("a", b, g, u + 1))
                        dve.tensor_tensor(roped[:, u % 3, :], roped[:, u % 3, :], sines[:, u % 2, :], ALU.add)\
                            .then_inc(rope_sum.sem, 1)

                    def rope_low(u):
                        dve.wait_ge(rope_hi.sem, rope_hi.at("a", b, g, u + 1))
                        dst, high = (kT[1][:, :], kT[0][:, :]) if u == 0 else (qT[1][:, u - 1, :], qT[0][:, u - 1, :])
                        low(dst, roped[:, u % 3, :], high).then_inc(rope_lo.sem, 1)

                    cosine(0, 0)
                    cosine(1, 1)
                    rotate(0, 0)
                    cosine(2, 2)
                    rotate(1, 1)
                    rope_low(0)
                    dve.wait_ge(proj.sem, proj.at("a", b, g, 4))
                    dve.tensor_copy(vT[:, :], proj_ps[1][:, :]).then_inc(proj_free.sem, 1)
                    cosine(3, 4)
                    rotate(2, 2)
                    rope_low(1)
                    cosine(4, 5)
                    rotate(3, 4)
                    rope_low(2)
                    for n in range(2):
                        dve.wait_ge(v_hi.sem, v_hi.at("a", b, g, n + 1))
                        low(v[1][:, 2 * n:2 * n + 2, :], proj_ps[n][:, 0:2 * P].rearrange("p (t e) -> p t e", t=2),
                            v[0][:, 2 * n:2 * n + 2, :]).then_inc(proj_free.sem, 1)
                        if n == 0:
                            rotate(4, 5)
                            rope_low(3)
                    rope_low(4)
                    dve.wait_ge(decay_in.sem, decay_in.at("a", b, g, 16))

                    def accumulate(t):
                        dve.wait_ge(y.sem, y.at("a", b, g, t + 1))
                        dve.tensor_tensor(y_acc[:, t, :], y_ps[t % 2][:, :], y_acc[:, t, :], ALU.add)\
                            .then_inc(y_free.sem, 1)
                        if following[0] == "b":
                            dve.wait_ge(y_free.sem, y_free.at("a", b, g, t + 1))
                            for k in HANDOVER_AT[t]:
                                handover("a", "b", NT, b, k)

                    dve.wait_ge(cleared.sem, cleared.at("a", b, None, 1))
                    dve.wait_ge(y_free.sem, y_free.at("a", b, g, 0))
                    for n in range(NBLK + LAG):
                        if n < NBLK:
                            i, j = BLOCKS[n]
                            dve.wait_ge(p_lo.sem, p_lo.at("a", b, g, n - 1))
                            dve.wait_ge(score.sem, score.at("a", b, g, n + 1))
                            dve.tensor_tensor(pf[:, n % 2, :].rearrange("p (h i) -> p h i", h=HG),
                                              score_ps[n % 2][:, :].rearrange("p (h i) -> p h i", h=HG),
                                              dec[:, :, i - j, :], ALU.mult).then_inc(p_f.sem, 1)
                            part, c = SPLIT_AT.get(n, (None, 0))
                            if part == 1:
                                split(1, "a", b, g, c)
                            elif part == 0 and c < CHUNKS[0][following[0]]:
                                split(0, following[0], b, following[1], c)
                        if n - LAG in LAST:
                            i = LAST.index(n - LAG)
                            dve.wait_ge(o_hi.sem, o_hi.at("a", b, g, i + 1))
                            low(oT[1][:, :, i * P:(i + 1) * P], o_ps[i % 2][:, :].rearrange("p (h i) -> p h i", h=HG),
                                oT[0][:, :, i * P:(i + 1) * P]).then_inc(o_free.sem, 1)
                        for t in WO_AFTER.get(n - LAG - 1, []):
                            accumulate(t)
                    for t in WO_AFTER[NBLK - 1]:
                        accumulate(t)

                with dve.Fori(0, KV0 - 1) as g:
                    a_step(g, ("a", g + 1))
                a_step(KV0 - 1, ("b", 0))
                for t in (NT - 2, NT - 1):
                    front_low("b", b, t)

                def b_step(g, following):
                    dve.wait_ge(scales_in.sem, scales_in.at("b", b, None, 48))
                    dve.wait_ge(cleared.sem, cleared.at("b", b, None, 1))
                    for m in range(IC):
                        dve.wait_ge(h_lo.sem, h_lo.at("b", b, g, m - 1))
                        dve.wait_ge(score.sem, score.at("b", b, g, m + 1))
                        dve.wait_ge(proj_free.sem, proj_free.at("b", b, g, m + 1))
                        dve.scalar_tensor_tensor(hf[:, m % 2, :], score_ps[m % 2][:, :], usc[:, bass.ds(g * IC + m, 1)],
                                                 silu[:, m % 2, :], ALU.mult, ALU.mult).then_inc(h_f.sem, 1)
                        if m < CHUNKS[1]["b"]:
                            split(1, "b", b, g, m)
                    dve.wait_ge(y_free.sem, y_free.at("b", b, g, 0))
                    for t in range(NT):
                        dve.wait_ge(y.sem, y.at("b", b, g, t + 1))
                        dve.tensor_tensor(y_acc[:, t, :], y_ps[t % 2][:, :], y_acc[:, t, :], ALU.add)\
                            .then_inc(y_free.sem, 1)
                        if t < CHUNKS[0][following[0]]:
                            split(0, following[0], b, following[1], t)
                        if following[0] == "c":
                            dve.wait_ge(y_free.sem, y_free.at("b", b, g, t + 1))
                            dve.tensor_tensor(y_acc[:, t, :], y_acc[:, t, :], dsc[:, :], ALU.mult).then_inc(y_scaled.sem, 1)
                            dve.wait_ge(y_scaled.sem, y_scaled.at("b", b, None, t + 1))
                            for k in HANDOVER_AT[t]:
                                handover("b", "c", 3 * NT, b, k)

                with dve.Fori(0, NQ - 1) as g:
                    b_step(g, ("b", g + 1))
                b_step(NQ - 1, ("c", None))
                for t in (NT - 2, NT - 1):
                    front_low("c", b, t)
                dve.wait_ge(consts1_in.sem, consts1_in.at("c", b, None, 64))
                dve.wait_ge(pads.sem, pads.at("c", b, None, 5))

                def moves(t):
                    for u in (1, 3, 5):
                        dve.wait_ge(score.sem, score.at("pack", b, None, 6 * t + u + 1))
                        move_pack(dve.tensor_copy, t, u).then_inc(moved[1].sem, 1)

                def rotate_pairs(t, part, ps, lo_, nh):
                    cos_, sin_ = rope1[:, 2 * part, t, :], rope1[:, 2 * part + 1, t, :]
                    w = nh * HD1
                    a_, b_ = ra[:, lo_:lo_ + w], rb[:, lo_:lo_ + w]
                    dve.wait_ge(proj.sem, proj.at("qkv", b, None, 2 * t + part + 1))
                    dve.wait_ge(rot_lo.sem, rot_lo.at("c", b, None, 2 * t))
                    dve.wait_ge(rot_sum.sem, rot_sum.at("c", b, None, 2 * t))
                    dve.tensor_tensor(a_.rearrange("p (h d) -> p h d", h=nh), ps[:, 0:w].rearrange("p (h d) -> p h d", h=nh),
                                      cos_.unsqueeze(1).to_broadcast([P, nh, HD1]), ALU.mult)
                    pairs = [z.rearrange("p (h d two) -> p h d two", h=nh, two=2) for z in (b_, ps[:, 0:w])]
                    s2_ = sin_.rearrange("p (d two) -> p d two", two=2)
                    for e in range(2):
                        last = dve.tensor_tensor(pairs[0][:, :, :, e], pairs[1][:, :, :, 1 - e],
                                                 s2_[:, :, e].unsqueeze(1).to_broadcast([P, nh, HD1 // 2]), ALU.mult)
                        if e == 0:
                            continue
                        last.then_inc(proj_free.sem, 1) if part == 0 else last.then_inc(rot_k.sem, 1)
                    if part == 1:
                        dve.wait_ge(rot_k.sem, rot_k.at("c", b, None, t + 1))
                        dve.tensor_copy(V1[:, t, :, 0:HD1], ps[:, w:2 * w].rearrange("p (h d) -> p h d", h=nh))\
                            .then_inc(proj_free.sem, 1)
                    else:
                        dve.wait_ge(proj_free.sem, proj_free.at("qkv", b, None, 2 * t + 1))
                    dve.tensor_tensor(a_, a_, b_, ALU.add).then_inc(rot_sum.sem, 1)

                for t in range(NT):
                    rotate_pairs(t, 0, proj_ps[0], 0, H1)
                    rotate_pairs(t, 1, proj_ps[1], NR, KV1)
                    if t >= 1:
                        moves(t - 1)
                    q_, k_ = ra[:, 0:NR].rearrange("p (h d) -> p h d", h=H1), ra[:, NR:].rearrange("p (h d) -> p h d", h=KV1)
                    dve.wait_ge(rot_hi.sem, rot_hi.at("c", b, None, 4 * t + 2))
                    low(q_pack[:, :, 2 * HD1:3 * HD1], q_, q_pack[:, :, 0:HD1]).then_inc(rot_lo.sem, 1)
                    dve.wait_ge(rot_hi.sem, rot_hi.at("c", b, None, 4 * t + 4))
                    low(k_pack[:, :, :, HD1:2 * HD1], k_.unsqueeze(2).to_broadcast([P, KV1, 2, HD1]),
                        k_pack[:, :, :, 0:HD1]).then_inc(rot_lo.sem, 1)
                moves(NT - 1)
                for k in range(KV1 + 3):
                    for u in range(NS):
                        if k < KV1:
                            i, heads = S1_BANKS[u]
                            (q, n), w = heads[0], (i + 1) * P
                            dst = row_max[:, k, i, q, n:n + len(heads)]
                            src = score_ps[(k * NS + u) % 2][:, 0:len(heads) * w].rearrange("p (n s) -> p n s", s=w)
                            dve.wait_ge(score.sem, score.at("s1", b, None, k * NS + u + 1))
                            dve.reduce_max(dst, src, AX_X).then_inc(s_max.sem, 1)
                        if k < 2 and u in (4, 8):
                            split(1 - k, "cd"[k], b, None, u // 4 - 1)
                        g = k - 1
                        if u == 2 and 0 <= g < KV1:
                            dve.wait_ge(m_in.sem, m_in.at("c", b, None, 32 * max(g - 1, 0)))
                            dve.wait_ge(max_rows.sem, max_rows.at("c", b, None, g + 1))
                            dve.tensor_copy(maxT[:, g % 2, :], y_ps[0][0:4, :]).then_inc(maxT_done.sem, 1)
                        g = k - 3
                        if g >= 0 and u == 3:
                            dve.wait_ge(pv1.sem, pv1.at("c", b, None, (g + 1) * NT))
                            dve.tensor_copy(yT[:, g % 2, :], o_ps[g % 2][:, :]).then_inc(yT_done.sem, 1)
                        if g >= 0 and u == 8:
                            ps = y_ps[1][:, :].rearrange("p (i h d) -> p (i h) d", h=4, d=32)
                            dve.wait_ge(y_back.sem, y_back.at("c", b, None, g + 1))
                            dve.wait_ge(y1_done.sem, y1_done.at("c", b, None, g - 1))
                            dve.reciprocal(rden[:, g % 2, :], ps[:, :, HD1:HD1 + 1].rearrange("p n a -> p (n a)")).then_inc(den_done.sem, 1)
                            dve.wait_ge(den_done.sem, den_done.at("c", b, None, g + 1))
                            dve.tensor_tensor(y_acc[:, :, g * 4 * HD1:(g + 1) * 4 * HD1].rearrange("p i (h d) -> p i h d", h=4),
                                              ps[:, :, 0:HD1].rearrange("p (i h) d -> p i h d", h=4),
                                              rden[:, g % 2, :].rearrange("p (i h) -> p i h", h=4).unsqueeze(3)
                                              .to_broadcast([P, NT, 4, HD1]), ALU.mult).then_inc(y1_done.sem, 1)
                for t in range(NT):
                    front_low("y", b, t)
                for t in range(NT):
                    dve.wait_ge(y.sem, y.at("c", b, None, t + 1))
                    dve.tensor_copy(y_acc[:, t, :], y_ps[t % 2][:, :]).then_inc(y_free.sem, 1)
                    dve.wait_ge(y_free.sem, y_free.at("c", b, None, t + 1))
                    for k in HANDOVER_AT[t]:
                        handover("c", "d", 5 * NT, b, k)
                for t in (NT - 2, NT - 1):
                    front_low("d", b, t)
                for t in range(NT):
                    dve.wait_ge(y.sem, y.at("d", b, None, t + 1))
                    dve.tensor_tensor(y_acc[:, t, :], y_ps[t % 2][:, :], gate_bias[:, :], ALU.add).then_inc(y_free.sem, 1)

            def row_norm(stage, g, k, m, dst, src):
                dve.bn_stats(stats[0:R, 0, :], src).then_inc(row.sem, 1)
                dve.wait_ge(row.sem, row.at(stage, 0, g, k + 1))
                dve.sem_inc(s_carry, 1)
                dve.bn_aggr(moments[0:R, 0, :], stats[0:R, 0, :]).then_inc(row.sem, 1)
                dve.wait_ge(row_rstd.sem, row_rstd.at(stage, 0, g, m + 1))
                dve.tensor_scalar(dst, src, moments[0:R, 0, 0:1], rstd[0:R, 0:1], ALU.subtract, ALU.mult).then_inc(row.sem, 1)
                dve.wait_ge(row.sem, row.at(stage, 0, g, k + 3))

            def row_affine(stage, g, k, n):
                dve.tensor_tensor(rows[:, :], rows[:, :], row_consts[:, n, :], ALU.mult).then_inc(row.sem, 1)
                dve.wait_ge(row.sem, row.at(stage, 0, g, k + 1))
                dve.tensor_tensor(rows[:, :], rows[:, :], row_consts[:, n + 1, :], ALU.add).then_inc(row.sem, 1)

            def rows_T(stage, g, mm):
                dve.wait_ge(row_mm.sem, row_mm.at(stage, 0, g, mm))
                dve.tensor_copy(rowsT[:, :, :].rearrange("p c r -> p (c r)"), o_ps[0][:, 0:KD * R]).then_inc(row.sem, 1)

            dve.wait_ge(row_in, ROW_INS)
            row_norm("pre", None, 0, 0, rows[:, :], rows[:, :])
            row_norm("pre", None, 3, 1, rows[:, :], rows[:, :])
            row_affine("pre", None, 6, 0)
            rows_T("pre", None, 1)
            dve.wait_ge(row_mm.sem, row_mm.at("pre", 0, None, 2))
            dve.tensor_tensor(thought[:, :], o_ps[1][0:R, :], row_consts[:, 2, :], ALU.add).then_inc(row.sem, 1)
            with dve.Fori(0, K_STEPS) as g:
                dve.wait_ge(row.sem, row.at("step", 0, g, 0))
                row_norm("step", g, 0, 0, rows[:, :], thought[:, :])
                row_affine("step", g, 3, 3)
                rows_T("step", g, 1)
                dve.wait_ge(row_mm.sem, row_mm.at("step", 0, g, 2))
                dve.tensor_tensor(hidden, score_ps[0][:, :], bias1[:, :], ALU.add).then_inc(row.sem, 1)
                dve.wait_ge(row_mm.sem, row_mm.at("step", 0, g, 3))
                dve.tensor_copy(hiddenT[:, :, :].rearrange("p c r -> p (c r)"), score_ps[1][:, :]).then_inc(row.sem, 1)
                dve.wait_ge(row_mm.sem, row_mm.at("step", 0, g, 4))
                dve.tensor_copy(partial, proj_ps[0][:, :]).then_inc(row.sem, 1)
                dve.wait_ge(row_mm.sem, row_mm.at("step", 0, g, 5))
                dve.tensor_tensor(rows[:, :], proj_ps[1][0:R, :], row_consts[:, 5, :], ALU.add).then_inc(row.sem, 1)
                dve.wait_ge(row.sem, row.at("step", 0, g, 10))
                dve.tensor_tensor(thought[:, :], thought[:, :], rows[:, :], ALU.add).then_inc(row.sem, 1)
            rows_T("post", None, 1)
            dve.wait_ge(row_mm.sem, row_mm.at("post", 0, None, 2))
            dve.tensor_tensor(rows[:, :], o_ps[1][0:R, :], row_consts[:, 6, :], ALU.add).then_inc(row.sem, 1)

            dve.wait_ge(d_in, 32)
            with dve.Fori(0, NB) as b:
                for t in range(NT):
                    def step(k):
                        dve.wait_ge(fin_step.sem, fin_step.at("o", b, None, 14 * t + k))

                    def fin_norm(k, m, dst, src):
                        n = 3 * t + m
                        dve.bn_stats(stats[:, n, :], src).then_inc(fin_step.sem, 1)
                        step(k + 1)
                        dve.sem_inc(s_carry, 1)
                        dve.bn_aggr(moments[:, n, :], stats[:, n, :]).then_inc(fin_step.sem, 1)
                        dve.wait_ge(fin_rstd.sem, fin_rstd.at("o", b, None, n + 1))
                        dve.tensor_scalar(dst, src, moments[:, n, 0:1], rstd[:, n:n + 1], ALU.subtract, ALU.mult)\
                            .then_inc(fin_step.sem, 1)
                        step(k + 3)

                    z, gate = Z[:, t, :], G[:, t, :]
                    dve.wait_ge(bc_in.sem, bc_in.at("o", b, None, 16))
                    dve.wait_ge(x3_in[t].sem, x3_in[t].at("o", b, None, 32))
                    fin_norm(0, 0, z, X[:, t, :])
                    dve.tensor_tensor(gate, gate, bcast[:, 0, :], ALU.mult).then_inc(fin_step.sem, 1)
                    step(4)
                    dve.tensor_tensor(z, z, gate, ALU.add).then_inc(fin_step.sem, 1)
                    step(5)
                    fin_norm(5, 1, z, z)
                    dve.tensor_tensor(z, z, gam[:, :], ALU.mult).then_inc(fin_step.sem, 1)
                    step(9)
                    dve.tensor_tensor(z, z, bet[:, :], ALU.add).then_inc(fin_step.sem, 1)
                    step(10)
                    fin_norm(10, 2, z, z)
                    dve.tensor_tensor(z, z, X[:, t, :], ALU.add).then_inc(fin_step.sem, 1)

        @block.tensor
        def _(pe):
            pe.sem_inc(y.sem, 1)
            pe.sem_inc(pv_done.sem, 4)
            pe.sem_inc(pv1.sem, 4)
            pe.wait_ge(s_ident, 16)

            def product(dst, terms):
                n = 3 * len(terms)
                k = 0
                for stat, mov in terms:
                    for s_, m_ in ((0, 0), (1, 0), (0, 1)):
                        last = pe.matmul(dst, stat[s_], mov[m_], start=(k == 0), stop=(k == n - 1))
                        k += 1
                return last

            def front(stage, b):
                for t in range(NT):
                    pe.wait_ge(proj_free.sem, proj_free.at("front_" + stage, b, None, t - 1))
                    if stage == "y":
                        pe.wait_ge(y1_done.sem, y1_done.at("c", b, None, KV1))
                    else:
                        n = t if stage == "a" else {"b": NT, "c": 3 * NT, "d": 5 * NT}[stage] + HANDOVER.index(("pre", t))
                        pe.wait_ge(ln_out.sem, ln_out.at("ln", b, None, n + 1))
                    src = y_acc[:, t, :] if stage == "y" else xn[:, t % 2, :]
                    for c in range(KD):
                        last = pe.transpose(proj_ps[t % 2][:, c * P:(c + 1) * P], src[:, c * P:(c + 1) * P],
                                            ident[:, :])
                    last.then_inc(proj.sem, 1)

            with pe.Fori(0, NB) as b:
                front("a", b)
                with pe.Fori(0, KV0) as g:
                    pe.wait_ge(proj_free.sem, proj_free.at("a", b, g, 0))
                    pe.wait_ge(w_lo[0].sem, w_lo[0].at("a", b, g, CHUNKS[0]["a"]))

                    def project(use, w):
                        pe.wait_ge(proj_free.sem, proj_free.at("a", b, g, use - 1))
                        product(proj_ps[use % 2][:, :],
                                [([w(W[s_], c) for s_ in range(2)], [XnT[m_][:, c, :] for m_ in range(2)])
                                 for c in range(KD)]).then_inc(proj.sem, 1)

                    project(0, wk)
                    project(1, lambda t, c: wq(t, c, 0))
                    project(2, lambda t, c: wq(t, c, 1))
                    project(3, wv)
                    project(4, lambda t, c: wq(t, c, 2))
                    project(5, lambda t, c: wq(t, c, 3))
                    for n in range(2):
                        pe.wait_ge(proj_free.sem, proj_free.at("a", b, g, 6 + n - 1))
                        for t in range(2):
                            last = pe.transpose(proj_ps[n][:, t * P:(t + 1) * P], vT[:, (2 * n + t) * P:(2 * n + t + 1) * P],
                                                ident[:, :])
                        last.then_inc(proj.sem, 1)
                    pe.wait_ge(rope_lo.sem, rope_lo.at("a", b, g, NU))

                    for n in range(NBLK + LAG):
                        if n < NBLK:
                            i, j = BLOCKS[n]
                            pe.wait_ge(p_f.sem, p_f.at("a", b, g, n - 1))
                            product(score_ps[n % 2][:, :].rearrange("p (h i) -> p h i", h=HG),
                                    [([kT[s_][:, j * P:(j + 1) * P] for s_ in range(2)],
                                      [qT[m_][:, :, i * P:(i + 1) * P] for m_ in range(2)])]).then_inc(score.sem, 1)
                        m = n - LAG
                        if m >= 0:
                            i, j = BLOCKS[m]
                            if m == 0:
                                pe.wait_ge(proj_free.sem, proj_free.at("a", b, g, PROJ_A))
                            if j == 0:
                                pe.wait_ge(o_free.sem, o_free.at("a", b, g, i - 1))
                            pe.wait_ge(p_lo.sem, p_lo.at("a", b, g, m + 1))
                            for k, (s_, m_) in enumerate(((0, 0), (1, 0), (0, 1))):
                                last = pe.matmul(o_ps[i % 2][:, :], v[s_][:, j, :], pT[m_][:, m % 4, :],
                                                 start=(j == 0 and k == 0), stop=(j == i and k == 2))
                            last.then_inc(pv_done.sem, 1)
                        for t in WO_AFTER.get(m, []):
                            if t == 0:
                                pe.wait_ge(w_lo[1].sem, w_lo[1].at("a", b, g, CHUNKS[1]["a"]))
                            pe.wait_ge(o_free.sem, o_free.at("a", b, g, t + 1))
                            pe.wait_ge(y_free.sem, y_free.at("a", b, g, t - 1))
                            product(y_ps[t % 2][:, :],
                                    [([oT[s_][:, h, t * P:(t + 1) * P] for s_ in range(2)],
                                      [wo(W[m_], h) for m_ in range(2)]) for h in range(HG)]).then_inc(y.sem, 1)
                front("b", b)
                with pe.Fori(0, NQ) as g:
                    pe.wait_ge(proj_free.sem, proj_free.at("b", b, g, 0))
                    pe.wait_ge(w_lo[0].sem, w_lo[0].at("b", b, g, CHUNKS[0]["b"]))
                    for m in range(IC):
                        for w, ps, free, done in ((wup, score_ps, h_f, score), (wgate, proj_ps, proj_free, proj)):
                            pe.wait_ge(free.sem, free.at("b", b, g, m - 1))
                            product(ps[m % 2][:, :],
                                    [([w(W[s_], c, m) for s_ in range(2)], [XnT[m_][:, c, :] for m_ in range(2)])
                                     for c in range(KD)]).then_inc(done.sem, 1)
                    pe.wait_ge(w_lo[1].sem, w_lo[1].at("b", b, g, CHUNKS[1]["b"]))
                    pe.wait_ge(h_lo.sem, h_lo.at("b", b, g, IC))
                    for t in range(NT):
                        pe.wait_ge(y_free.sem, y_free.at("b", b, g, t - 1))
                        product(y_ps[t % 2][:, :],
                                [([hT[s_][:, m, t * P:(t + 1) * P] for s_ in range(2)],
                                  [wo(W[m_], m) for m_ in range(2)]) for m in range(IC)]).then_inc(y.sem, 1)
                front("c", b)
                pe.wait_ge(proj_free.sem, proj_free.at("front_c", b, None, NT))
                pe.wait_ge(w_lo[0].sem, w_lo[0].at("c", b, None, CHUNKS[0]["c"]))

                def packs(t):
                    pe.wait_ge(rot_lo.sem, rot_lo.at("c", b, None, 2 * t + 2))
                    for u in range(6):
                        pe.wait_ge(moved[u % 2].sem, moved[u % 2].at("c", b, None, 3 * t + u // 2))
                        for n in range(4):
                            src = q_pack[:, 2 * (4 * u + n):2 * (4 * u + n) + 2, :].rearrange("p h d -> p (h d)") if u < 4 \
                                else k_pack[:, 4 * (u - 4) + n, :, :].rearrange("p a d -> p (a d)")
                            last = pe.transpose(score_ps[u % 2][:, n * P:(n + 1) * P], src.bitcast(F32), ident[:, :])
                        last.then_inc(score.sem, 1)

                for t in range(NT):
                    for part, w in enumerate((wq1, wkv1)):
                        width = w(W[0], 0).shape[1]
                        pe.wait_ge(proj_free.sem, proj_free.at("qkv", b, None, 2 * t + part - 1))
                        product(proj_ps[part][:, 0:width],
                                [([XnT[s_][:, c, t * P:(t + 1) * P] for s_ in range(2)], [w(W[m_], c) for m_ in range(2)])
                                 for c in range(KD)]).then_inc(proj.sem, 1)
                    if t >= 1:
                        packs(t - 1)
                packs(NT - 1)
                for n in range(2):
                    pe.wait_ge(moved[n].sem, moved[n].at("c", b, None, 3 * NT))

                def scores(k, u):
                    i, heads = S1_BANKS[u]
                    w, n = (i + 1) * P, k * NS + u
                    ps = score_ps[n % 2]
                    pe.wait_ge(s_max.sem, s_max.at("c", b, None, n - 1))
                    for m, (q, pair) in enumerate(heads):
                        rows = slice(64 * q, 64 * q + 64)
                        pe.matmul(ps[:, m * w:(m + 1) * w], QT[rows, 2 * k + pair, i * P:(i + 1) * P], KT[rows, k, 0:w],
                                  start=(m == 0), stop=False, skip_group_check=True)
                    dst = ps[:, 0:len(heads) * w].rearrange("p (h s) -> p h s", s=w)[:, :, i * P:w]
                    pe.matmul(dst, ident_b[:, :], mask[:, :].unsqueeze(1).to_broadcast([P, len(heads), P]),
                              start=False, stop=True, skip_group_check=True).then_inc(score.sem, 1)

                def scores_T(g, u):
                    j, heads = S2_BANKS[u]
                    w, n = S - j * P, g * NS + u
                    if u == 0:
                        pe.wait_ge(m_in.sem, m_in.at("c", b, None, 32 * (g + 1)))
                    pe.wait_ge(proj_free.sem, proj_free.at("s2", b, None, n - 1))
                    for m, (q, pair) in enumerate(heads):
                        rows = slice(64 * q, 64 * q + 64)
                        last = pe.matmul(proj_ps[n % 2][:, m * w:(m + 1) * w], KT[rows, g, j * P:(j + 1) * P],
                                         QT[rows, 2 * g + pair, j * P:S], start=True, stop=True)
                    last.then_inc(proj.sem, 1)

                def values(g, j):
                    if j == 0:
                        pe.wait_ge(yT_done.sem, yT_done.at("c", b, None, g - 1))
                    pe.wait_ge(masked.sem, masked.at("c", b, None, g * NT + j + 1))
                    for m, (q, pair) in enumerate(HEADS1):
                        at = 32 * (2 * pair + q)
                        last = pe.matmul(o_ps[g % 2][at:at + 32, j * P:S], V1[:, j, g, :], probs[j][:, m, :],
                                         start=(j == 0), stop=(j == NT - 1), skip_group_check=True)
                    last.then_inc(pv1.sem, 1)

                for k in range(KV1 + 3):
                    for u in range(NS):
                        if k < KV1:
                            scores(k, u)
                        g = k - 1
                        if u == 1 and 0 <= g < KV1:
                            pe.wait_ge(s_max.sem, s_max.at("c", b, None, (g + 1) * NS))
                            pe.wait_ge(maxT_done.sem, maxT_done.at("c", b, None, g)) if g >= 1 else None
                            for i in range(NT):
                                last = pe.matmul(y_ps[0][0:4, i * P:(i + 1) * P],
                                                 row_max[:, g, i, :, :].rearrange("p q n -> p (q n)"), ident[:, :],
                                                 start=True, stop=True)
                            last.then_inc(max_rows.sem, 1)
                        g = k - 2
                        if 0 <= g < KV1:
                            scores_T(g, u)
                            if u == 6:
                                values(g, 0)
                            if u == 9:
                                values(g, 1)
                        g = k - 3
                        if g >= 0:
                            if u == 0:
                                values(g, 2)
                            if u == 2:
                                values(g, 3)
                            if u == 5:
                                pe.wait_ge(yT_done.sem, yT_done.at("c", b, None, g + 1))
                                pe.wait_ge(y1_done.sem, y1_done.at("c", b, None, g))
                                for i in range(NT):
                                    last = pe.transpose(y_ps[1][:, i * P:(i + 1) * P], yT[:, g % 2, i * P:(i + 1) * P],
                                                        ident[:, :])
                                last.then_inc(y_back.sem, 1)
                front("y", b)
                pe.wait_ge(proj_free.sem, proj_free.at("front_y", b, None, NT))
                pe.wait_ge(w_lo[1].sem, w_lo[1].at("c", b, None, CHUNKS[1]["c"]))
                for t in range(NT):
                    pe.wait_ge(y_free.sem, y_free.at("c", b, None, t - 1))
                    product(y_ps[t % 2][:, :],
                            [([XnT[s_][:, c, t * P:(t + 1) * P] for s_ in range(2)], [wo(W[m_], c) for m_ in range(2)])
                             for c in range(KD)]).then_inc(y.sem, 1)
                front("d", b)
                pe.wait_ge(proj_free.sem, proj_free.at("front_d", b, None, NT))
                pe.wait_ge(w_lo[0].sem, w_lo[0].at("d", b, None, CHUNKS[0]["d"]))
                for t in range(NT):
                    pe.wait_ge(y_free.sem, y_free.at("d", b, None, t - 1))
                    product(y_ps[t % 2][:, :],
                            [([XnT[s_][:, c, t * P:(t + 1) * P] for s_ in range(2)],
                              [W[m_][:, c * D:(c + 1) * D] for m_ in range(2)]) for c in range(KD)]).then_inc(y.sem, 1)

            def rows_T(stage, g, src, k):
                pe.wait_ge(row.sem, row.at(stage, 0, g, k))
                for c in range(KD):
                    last = pe.matmul(o_ps[0][:, c * R:(c + 1) * R], src[:, c * P:(c + 1) * P], ident[0:R, 0:R],
                                     start=True, stop=True)
                last.then_inc(row_mm.sem, 1)
                pe.wait_ge(row.sem, row.at(stage, 0, g, k + 1))

            def linear(w):
                for c in range(KD):
                    last = pe.matmul(o_ps[1][0:R, :], rowsT[:, c, :], w[:, c, :], start=(c == 0), stop=(c == KD - 1))
                last.then_inc(row_mm.sem, 1)

            rows_T("pre", None, rows, 8)
            linear(aggw)
            with pe.Fori(0, K_STEPS) as g:
                rows_T("step", g, rows, 5)
                for c in range(KD):
                    for n in range(4):
                        last = pe.matmul(score_ps[0][R * n:R * n + R, :], rowsT[:, c, :], d1w[:, c, n * D:(n + 1) * D],
                                         start=(c == 0), stop=(c == KD - 1), skip_group_check=True)
                last.then_inc(row_mm.sem, 1)
                pe.wait_ge(gelu_done.sem, gelu_done.at("step", 0, g, 1))
                for c in range(KD):
                    last = pe.transpose(score_ps[1][:, c * P:(c + 1) * P], hidden[:, c * P:(c + 1) * P], ident[:, :])
                last.then_inc(row_mm.sem, 1)
                pe.wait_ge(row.sem, row.at("step", 0, g, 8))
                for c in range(KD):
                    for n in range(4):
                        last = pe.matmul(proj_ps[0][R * n:R * n + R, :], hiddenT[:, c, R * n:R * n + R], d2w[:, n * KD + c, :],
                                         start=(c == 0), stop=(c == KD - 1), skip_group_check=True)
                last.then_inc(row_mm.sem, 1)
                pe.wait_ge(row.sem, row.at("step", 0, g, 9))
                pe.matmul(proj_ps[1][0:R, :], summing[:, :], partial, start=True, stop=True).then_inc(row_mm.sem, 1)
            rows_T("post", None, thought, 0)
            linear(bcw)


def rope0_tables():
    import numpy as np
    inv = np.float32(1) / np.float32(10000) ** (np.arange(0, DH0, 2, dtype=np.float32) / np.float32(DH0))
    ang = (np.arange(S, dtype=np.float32)[:, None] * inv[None, :].astype(np.float32)).T
    cos, sin = np.cos(ang), np.sin(ang)
    return (np.concatenate([cos, cos]).astype(np.float32), np.concatenate([-sin, sin]).astype(np.float32))


def rope1_table():
    import numpy as np
    inv = np.float32(1) / np.float32(10000) ** (np.arange(0, HD1, 2, dtype=np.float32) / np.float32(HD1))
    ang = np.arange(S, dtype=np.float32)[:, None] * inv[None, :].astype(np.float32)
    cos = np.repeat(np.cos(ang), 2, axis=1)
    sin = np.stack([-np.sin(ang), np.sin(ang)], axis=2).reshape(S, HD1)
    scale = np.float32(HD1 ** -0.5)
    t = np.stack([cos * scale, sin * scale, cos, sin]).reshape(4, NT, P, HD1).transpose(2, 0, 1, 3)
    return np.ascontiguousarray(t.reshape(P, 4 * NT * HD1).astype(np.float32))


def decay_table():
    import numpy as np
    lam = np.exp2(np.float32(-8) * np.arange(1, H0 + 1, dtype=np.float32) / np.float32(H0)).astype(np.float32)
    diff = (np.arange(NT)[:, None] * P + np.arange(P)[None, :])[None] - np.arange(P)[:, None, None]
    diff = diff.astype(np.float32)
    t = np.where(diff[None] >= 0, np.exp(-lam[:, None, None, None] * np.maximum(diff[None], 0)), 0)
    t = t.reshape(KV0, HG, P, NT, P).transpose(0, 2, 1, 3, 4)
    return np.ascontiguousarray(t.reshape(KV0, P, HG * NT * P).astype(np.float32))


def kernel(**inputs):
    import ml_dtypes
    import numpy as np
    import concourse.bacc as bacc
    from concourse.bass_utils import run_bass_kernel_spmd

    a = {k: np.asarray(v) for k, v in inputs.items()}

    def rows(w, n, per):
        return w.reshape(n, per, KD, P).transpose(0, 3, 2, 1).reshape(n, P, KD * per)

    def cols(w, n):
        k = w.shape[1] // n // P
        return w.T.reshape(n, k, P, w.shape[0]).transpose(0, 2, 1, 3).reshape(n, P, k * w.shape[0])

    def blocks(w):
        return w.reshape(-1, P, w.shape[1]).transpose(1, 0, 2)

    cos0, sin0 = rope0_tables()
    arrays = {
        "x": a["L0_attn_x"],
        "w_a": np.concatenate([rows(a["L0_attn_wk"], KV0, P), rows(a["L0_attn_wv"], KV0, P),
                               rows(a["L0_attn_wq"], KV0, HG * P), cols(a["L0_attn_wo"], KV0)], axis=2),
        "w_b": np.concatenate([rows(a["L0_ffn_up_w"], NQ, I0 // NQ), rows(a["L0_ffn_gate_w"], NQ, I0 // NQ),
                               cols(a["L0_ffn_down_w"], NQ)], axis=2),
        "gate_scale": a["L0_ffn_gate_scale"].reshape(I0 // P, P).T,
        "up_scale": a["L0_ffn_up_scale"].reshape(I0 // P, P).T,
        "down_scale": a["L0_ffn_down_scale"],
        "rope0_cos": cos0, "rope0_sin": sin0, "decay": decay_table(),
        "identity": np.eye(P, dtype=np.float32),
        "w_c": np.concatenate([
            np.concatenate([rows(a["L1_attn_wk"], 1, P).reshape(P, KD, P),
                            rows(a["L1_attn_wv"], 1, P).reshape(P, KD, P)], axis=2).reshape(1, P, KD * 2 * P),
            rows(a["L1_attn_wq"], 1, D), cols(a["L1_attn_wo"], 1)], axis=2),
        "rope1_tables": rope1_table(),
        "w_gate": blocks(a["L1_ffn_gate_w"]).reshape(P, KD * D), "agg_w": blocks(a["L1_ffn_agg_w"]),
        "bc_w": blocks(a["L1_ffn_bc_w"]), "d1_w": blocks(a["L1_ffn_d1_w"]), "d2_w": blocks(a["L1_ffn_d2_w"]),
        **{n: a["L1_ffn_" + n] for n in ("gate_b", "in_gamma", "in_beta", "agg_b", "pn_gamma", "pn_beta", "d1_b",
                                         "d2_b", "bc_b", "out_gamma", "out_beta")},
        "row_sum": np.tile(np.eye(R, dtype=np.float32), (P // R, 1)),
        "causal": np.triu(np.full((P, P), MASKED, np.float32), 1).astype(ml_dtypes.bfloat16),
        "identity_b": np.eye(P, dtype=np.float32).astype(ml_dtypes.bfloat16),
    }
    arrays = {k: np.ascontiguousarray(v) for k, v in arrays.items()}
    nc = bacc.Bacc("TRN2", target_bir_lowering=False, num_devices=1)
    args = {k: nc.dram_tensor(k, v.shape, mybir.dt.from_np(v.dtype), kind="ExternalInput").ap()
            for k, v in arrays.items()}
    out = nc.dram_tensor("out", arrays["x"].shape, F32, kind="ExternalOutput").ap()
    build(nc, out=out, **args)
    r = run_bass_kernel_spmd(nc, [arrays], core_ids=[0])
    return r.results[0]["out"]
```

```python
from contextlib import ExitStack

import concourse.bass as bass
from concourse import mybir

ALU = mybir.AluOpType
ACT = mybir.ActivationFunctionType
F32 = mybir.dt.float32
F32R = mybir.dt.float32r
BF16 = mybir.dt.bfloat16
I32 = mybir.dt.int32
AX_X = mybir.AxisListType.X

P = 128
S = 512
D = 512
KD = D // P
NT = S // P
H0, KV0, DH0 = 16, 4, 128
HG = H0 // KV0
I0 = 2048
NQ = 4
IC = I0 // NQ // P
H1, KV1, HD1 = 32, 8, 16
LN_EPS = 1e-5
ZERO_POINT = 128.0
BLOCKS = [(i, j) for i in range(NT) for j in range(i + 1)]
NBLK = len(BLOCKS)
LAG = 3
HEADS1 = [(q, n) for q in range(2) for n in range(2)]
SINGLE, DOUBLE = [[h] for h in HEADS1], [HEADS1[:2], HEADS1[2:]]
S1_BANKS = [(i, hs) for i, sets in ((0, DOUBLE), (1, DOUBLE), (2, SINGLE), (3, SINGLE)) for hs in sets]
S2_BANKS = [(j, hs) for j, sets in ((0, SINGLE), (1, SINGLE), (2, DOUBLE), (3, DOUBLE)) for hs in sets]
NS = len(S1_BANKS)
K_STEPS = 4
EPS_FFN = 1e-6
R = 32
ROW_M = 48
MASKED = -1e30


class Signal:

    def __init__(self, semaphore, stages, credit=0):
        self.sem, self.credit, self.offset, self.per = semaphore, credit, {}, {}
        at = 0
        for name, per, inner in stages:
            self.offset[name], self.per[name] = at, per
            at += per * inner
        self.total = at

    def at(self, stage, b, g, k):
        value = self.offset[stage] + k + self.credit
        if self.total:
            value = b * self.total + value
        return value if g is None else g * self.per[stage] + value


W_COLS = 6144
PIECE = (0, 4096)
CHUNK = 1024
CHUNKS = ({"a": 3, "b": 4, "c": 3, "d": 2}, {"a": 2, "b": 2, "c": 2})
SPLIT_AT = {2: 0, 4: 1, 6: 2, 7: 3}
HANDOVER = [("post", 0), ("post", 1), ("post", 2), ("pre", 0), ("post", 3), ("pre", 1), ("pre", 2), ("pre", 3)]
assert len(HANDOVER) == 2 * NT


def build(nc, x, w_a, w_b, gate_scale, up_scale, down_scale,
          w_c, rope1_tables, causal, identity_b,
          w_gate, gate_b, agg_w, d1_w, d2_w, bc_w, in_gamma, in_beta, agg_b, pn_gamma, pn_beta, d1_b, d2_b,
          bc_b, out_gamma, out_beta, row_sum,
          rope0_cos, rope0_sin, decay, identity, out):
    NB = x.shape[0]
    x3_dram = nc.dram_tensor("x3_dram", [NB, S, D], F32, kind="Internal").ap()
    gate_dram = nc.dram_tensor("gate_dram", [NB, S, D], F32, kind="Internal").ap()
    bc_dram = nc.dram_tensor("bc_dram", [NB, D], F32, kind="Internal").ap()
    NL = 7 * NT

    with ExitStack() as ctx:
        def sb(name, shape, dt=F32, c=ctx):
            return c.enter_context(nc.sbuf_tensor(name, shape, dt))

        def sem(name):
            return ctx.enter_context(nc.semaphore(name))

        def signal(name, stages, credit=0):
            return Signal(sem(name), stages, credit)

        X = sb("X", [P, NT, D])
        xn = sb("xn", [P, 2, D])
        XnT = [sb(f"XnT_{n}", [P, KD, S], F32R) for n in ("hi", "lo")]
        w_raw = sb("w_raw", [P, W_COLS])
        W = [sb(f"w_{n}", [P, W_COLS], F32R) for n in ("hi", "lo")]
        y_acc = sb("y_acc", [P, NT, D])
        ident = sb("ident", [P, P])
        eps, minus_half = sb("eps", [P, 1]), sb("minus_half", [P, 1])
        stats, moments = sb("stats", [P, NL, 6]), sb("moments", [P, NL, 2])
        var_eps, rstd = sb("var_eps", [P, NL]), sb("rstd", [P, NL])

        def ring(name):
            return [ctx.enter_context(nc.psum_tensor(f"{name}{n}", [P, 512], F32)) for n in range(2)]

        proj_ps, score_ps, o_ps, y_ps = ring("proj_ps"), ring("score_ps"), ring("o_ps"), ring("y_ps")

        PROJ_A = 4 + HG
        in_proj = [("front_a", NT, 1), ("a", PROJ_A, KV0), ("front_b", NT, 1), ("b", IC, NQ),
                   ("front_c", NT, 1), ("qkv", 2 * NT, 1), ("s2", NS * KV1, 1), ("front_y", NT, 1),
                   ("front_d", NT, 1)]
        in_score = [("a", NBLK, KV0), ("b", IC, NQ), ("pack", 6 * NT, 1), ("s1", NS * KV1, 1)]
        in_y = [("a", NT, KV0), ("b", NT, NQ), ("c", NT, 1), ("d", NT, 1)]
        proj, proj_free = signal("s_proj", in_proj), signal("s_proj_free", in_proj, 2)
        score = signal("s_score", in_score)
        o_free = signal("s_o_free", [("a", NT, KV0)], 2)
        y, y_free = signal("s_y", in_y, 1), signal("s_y_free", in_y, 2)

        in_ln = [("ln", NL, 1)]
        ln_stats, ln_moments, ln_var, ln_rstd = (signal(n, in_ln) for n in (
            "s_ln_stats", "s_ln_moments", "s_ln_var", "s_ln_rstd"))
        ln_out = signal("s_ln_out", in_ln, 1)
        front_hi = signal("s_front_hi", [(n, NT, 1) for n in ("a", "b", "c", "y", "d")])
        resid = signal("s_resid", [(n, NT, 1) for n in ("a", "b", "c")])
        cleared = signal("s_cleared", [("a", 1, 1), ("b", 1, 1)])

        inner = {"a": KV0, "b": NQ, "c": 1, "d": 1}
        in_w = [[(s_, n_, inner[s_]) for s_, n_ in CHUNKS[n].items()] for n in range(2)]
        w_in = [signal(f"s_w_in{n}", [(s_, 16, m_) for s_, _, m_ in in_w[n]]) for n in range(2)]
        w_hi = [signal(f"s_w_hi{n}", in_w[n]) for n in range(2)]
        w_lo = [signal(f"s_w_lo{n}", in_w[n], 1) for n in range(2)]
        s_pool_const, s_ident = sem("s_pool_const"), sem("s_ident")
        s_carry = sem("s_carry")
        x_in = signal("s_x_in", [("x", 16, 1)])
        x3_stored, gate_stored = signal("s_x3_stored", [("x", 16, 1)], 16), signal("s_gate_stored", [("x", 16, 1)], 16)
        gate_done = signal("s_gate", [("d", NT, 1)])

        A = ExitStack()
        cosT, sinT = sb("cosT", [P, S], c=A), sb("sinT", [P, S], c=A)
        dec = sb("dec", [P, HG, NT, P], c=A)
        qT = [sb(f"qT_{n}", [P, HG, S], F32R, A) for n in ("hi", "lo")]
        kT = [sb(f"kT_{n}", [P, S], F32R, A) for n in ("hi", "lo")]
        vT = sb("vT", [P, S], c=A)
        v = [sb(f"v_{n}", [P, NT, P], F32R, A) for n in ("hi", "lo")]
        swapped, sines = sb("swapped", [P, 2, S], c=A), sb("sines", [P, 2, S], c=A)
        roped = sb("roped", [P, 3, S], c=A)
        pf = sb("pf", [P, 2, 512], c=A)
        pT = [sb(f"pT_{n}", [P, 4, 512], F32R, A) for n in ("hi", "lo")]
        oT = [sb(f"oT_{n}", [P, HG, S], F32R, A) for n in ("hi", "lo")]
        A.close()
        NU = 1 + HG
        in_rope = [("a", NU, KV0)]
        tables_in = signal("s_tables_in", [("a", 32, 1)])
        decay_in = signal("s_decay_in", [("a", 16, KV0)])
        swap_done = signal("s_swap", [("a", 2 * NU, KV0)])
        sin_done, rope_hi = signal("s_sin", in_rope, 1), signal("s_rope_hi", in_rope)
        rope_sum, rope_lo = signal("s_rope_sum", in_rope, 1), signal("s_rope_lo", in_rope, 1)
        vT_done = signal("s_vT", [("a", 1, KV0)])
        v_hi, v_lo = signal("s_v_hi", [("a", 2, KV0)]), signal("s_v_lo", [("a", 2, KV0)])
        in_blk = [("a", NBLK, KV0)]
        p_f, p_hi = signal("s_p_f", in_blk, 2), signal("s_p_hi", in_blk)
        p_lo, pv_done = signal("s_p_lo", in_blk, 2), signal("s_pv", in_blk, 4)
        o_hi, o_lo = signal("s_o_hi", [("a", NT, KV0)]), o_free

        B = ExitStack()
        gsc, usc = sb("gsc", [P, I0 // P], c=B), sb("usc", [P, I0 // P], c=B)
        dsc = sb("dsc", [P, D], c=B)
        silu, hf = sb("silu", [P, 2, S], c=B), sb("hf", [P, 2, S], c=B)
        hT = [sb(f"hT_{n}", [P, IC, S], F32R, B) for n in ("hi", "lo")]
        B.close()
        scales_in = signal("s_scales_in", [("b", 48, 1)])
        in_h = [("b", IC, NQ)]
        h_f = signal("s_h_f", in_h, 2)
        h_hi, h_lo = signal("s_h_hi", in_h), signal("s_h_lo", in_h, 2)
        y_scaled = signal("s_y_scaled", [("b", NT, 1)])

        C = ExitStack()
        rope1 = sb("rope1", [P, 4, NT, HD1], c=C)
        mask = sb("mask", [P, P], BF16, C)
        ident_b = sb("ident_b", [P, P], BF16, C)
        ra, rb = sb("ra", [P, (H1 + KV1) * HD1], c=C), sb("rb", [P, (H1 + KV1) * HD1], c=C)
        q_pack = sb("q_pack", [P, H1, 64], F32R, C)
        k_pack = sb("k_pack", [P, KV1, 2, 64], F32R, C)
        QT = sb("QT", [P, H1 // 2, S], F32R, C)
        KT = sb("KT", [P, KV1, S], F32R, C)
        V1 = sb("V1", [P, NT, KV1, 32], c=C)
        row_max = sb("row_max", [P, KV1, NT, 2, 2], c=C)
        maxT = sb("maxT", [4, 2, S], F32R, C)
        probs = [sb(f"probs{j}", [P, 4, S - j * P], c=C) for j in range(NT)]
        yT = xn
        rden = sb("rden", [P, 2, NT * 4], c=C)
        gate_bias = sb("gate_bias", [P, D], c=C)
        C.close()
        NR, NQC = H1 * HD1, KV1 * HD1
        consts1_in = signal("s_consts1_in", [("c", 64, 1)])
        pads = signal("s_pads", [("c", 5, 1)])
        in_t = [("c", 2 * NT, 1)]
        rot_sum, rot_lo = signal("s_rot_sum", in_t, 1), signal("s_rot_lo", in_t, 1)
        rot_hi = signal("s_rot_hi", [("c", 4 * NT, 1)])
        rot_k = signal("s_rot_k", [("c", NT, 1)])
        moved = [signal(f"s_moved{n}", [("c", 3 * NT, 1)], 1) for n in range(2)]
        s_max = signal("s_max", [("c", NS * KV1, 1)], 2)
        in_g = [("c", KV1, 1)]
        max_rows, maxT_done = signal("s_max_rows", in_g), signal("s_maxT", in_g)
        m_in = signal("s_m_in", [("c", 32 * KV1, 1)], 16)
        masked, pv1 = signal("s_masked", [("c", NT * KV1, 1)]), signal("s_pv1", [("c", NT * KV1, 1)], 4)
        yT_done, y_back = signal("s_yT", in_g, 2), signal("s_y_back", in_g)
        den_done, y1_done = signal("s_den", in_g), signal("s_y1", in_g, 2)

        Dx = ExitStack()
        d1w, d2w = sb("d1w", [P, KD, I0], c=Dx), sb("d2w", [P, I0 // P, D], c=Dx)
        aggw, bcw = (w_raw[:, n * KD * D:(n + 1) * KD * D].rearrange("p (k n) -> p k n", k=KD) for n in range(2))
        row_consts = sb("row_consts", [R, 7, D], c=Dx)
        thought, rows = sb("thought", [R, D], c=Dx), sb("rows", [R, D], c=Dx)
        bias1, gam, bet = sb("bias1", [P, D], c=Dx), sb("gam", [P, D], c=Dx), sb("bet", [P, D], c=Dx)
        rowsT, hiddenT = sb("rowsT", [P, KD, R], c=Dx), sb("hiddenT", [P, KD, P], c=Dx)
        summing = sb("summing", [P, R], c=Dx)
        eps_ffn = sb("eps_ffn", [P, 1], c=Dx)
        bcast = sb("bcast", [P, 2, D], c=Dx)
        Dx.close()
        def by_block(cols):
            return cols.rearrange("p (t d) -> p t d", t=NT)

        X_, G_, Z_ = ((X[:, :, :], by_block(d1w[:, 0, :])),
                      (by_block(w_raw[:, 2 * KD * D:3 * KD * D]), by_block(d1w[:, 1, :])),
                      (y_acc[:, :, :], by_block(d1w[:, 2, :])))
        hidden, partial = xn[:, 0, :], xn[:, 1, :]
        row_in, d_in = sem("s_row_in"), sem("s_d_in")
        in_row = [("pre", 10, 1), ("step", 11, K_STEPS), ("post", 2, 1)]
        row = signal("s_row", in_row)
        row_mm = signal("s_row_mm", [("pre", 2, 1), ("step", 5, K_STEPS), ("post", 2, 1)])
        row_var, row_rstd = (signal(n, [("pre", 2, 1), ("step", 1, K_STEPS)]) for n in ("s_row_var", "s_row_rstd"))
        gelu_done = signal("s_gelu", [("step", 1, K_STEPS)])
        s_rows_clear, s_bc_out, s_eps2 = sem("s_rows_clear"), sem("s_bc_out"), sem("s_eps2")
        assert NB % 2 == 0
        x3_in = [[signal(f"s_x3_in{s_}{t}", [("o", 32, 1)]) for t in range(NT)] for s_ in range(2)]
        out_stored = [[signal(f"s_out_stored{s_}{t}", [("o", 16, 1)], 16) for t in range(NT)] for s_ in range(2)]
        bc_in = [signal(f"s_bc_in{s_}", [("o", 16, 1)]) for s_ in range(2)]
        fin_step = signal("s_fin_step", [("o", 11 * NT, 1)])
        fin_gate, fin_out = signal("s_fin_gate", [("o", NT, 1)]), signal("s_fin_out", [("o", NT, 1)])
        fin_var, fin_rstd = signal("s_fin_var", [("o", 3 * NT, 1)]), signal("s_fin_rstd", [("o", 3 * NT, 1)])

        block = ctx.enter_context(nc.Block())

        def wk(t, c):
            return t[:, c * P:(c + 1) * P]

        def wv(t, c):
            return t[:, (KD + c) * P:(KD + c + 1) * P]

        def wq(t, c, h):
            at = 2 * KD * P + c * HG * P + h * P
            return t[:, at:at + P]

        def wo(t, h):
            return t[:, PIECE[1] + h * D:PIECE[1] + (h + 1) * D]

        def wup(t, c, m):
            return t[:, c * 512 + m * P:c * 512 + (m + 1) * P]

        def wgate(t, c, m):
            return wup(t, KD + c, m)

        def chunk(t, n, c):
            return t[:, PIECE[n] + c * CHUNK:PIECE[n] + (c + 1) * CHUNK]

        def wkv1(t, c):
            return t[:, c * 2 * NQC:(c + 1) * 2 * NQC]

        def wq1(t, c):
            return t[:, KD * 2 * NQC + c * NR:KD * 2 * NQC + (c + 1) * NR]

        ROW_INS = 16 * 17
        W_A, W_B = (3072, 5120), (4096, 6144)
        S2_END = [sum(jj <= j for jj, _ in S2_BANKS) for j in range(NT)]
        LAST = [max(n for n, (i, j) in enumerate(BLOCKS) if i == q) for q in range(NT)]
        WO_AFTER = {LAST[1] + 2: [0], LAST[2] + 2: [1], LAST[3]: [2, 3]}
        WO_AFTER_BLOCK = {t: m + 1 for m, ts in WO_AFTER.items() for t in ts}

        @block.sync
        def _(sp):
            sp.dma_start(ident[:, :], identity).then_inc(s_ident, 16)
            sp.sem_inc(x3_stored.sem, 16)
            sp.sem_inc(m_in.sem, 16)
            with sp.Fori(0, NB) as b:
                def load(n, stage, g, src, ends, dt=F32):
                    start, lo, hi = PIECE[n], (0, ends[0])[n], ends[n]
                    step = src if g is None else src[bass.ds(g, 1), :, :]
                    sp.wait_ge(w_lo[n].sem, w_lo[n].at(stage, b, g, 0))
                    sp.dma_start(w_raw[:, start:start + hi - lo].bitcast(dt),
                                 step[:, :, lo:hi].rearrange("a p n -> (a p) n"))\
                        .then_inc(w_in[n].sem, 16)

                load(0, "a", 0, w_a, W_A)
                sp.wait_ge(x3_stored.sem, x3_stored.at("x", b, None, 0))
                sp.wait_ge(ln_out.sem, ln_out.at("ln", b, None, 0))
                sp.dma_start(X[:, :, :], x[bass.ds(b, 1), :, :].rearrange("a (t p) d -> p (a t) d", p=P))\
                    .then_inc(x_in.sem, 16)
                sp.wait_ge(y_free.sem, y_free.at("a", b, None, 0))
                sp.dma_start(cosT[:, :], rope0_cos).then_inc(tables_in.sem, 16)
                sp.dma_start(sinT[:, :], rope0_sin).then_inc(tables_in.sem, 16)

                def load_decay(g):
                    sp.wait_ge(p_f.sem, p_f.at("a", b, g, 0))
                    sp.dma_start(dec[:, :, :, :].rearrange("p h t i -> p (h t i)"),
                                 decay[bass.ds(g, 1), :, :].rearrange("a p n -> (a p) n"))\
                        .then_inc(decay_in.sem, 16)

                with sp.Fori(0, KV0 - 1) as g:
                    load(1, "a", g, w_a, W_A)
                    load_decay(g)
                    load(0, "a", g + 1, w_a, W_A)
                load(1, "a", KV0 - 1, w_a, W_A)
                load_decay(KV0 - 1)
                load(0, "b", 0, w_b, W_B, I32)
                sp.wait_ge(resid.sem, resid.at("a", b, None, NT))
                sp.dma_start(gsc[:, :], gate_scale).then_inc(scales_in.sem, 16)
                sp.dma_start(usc[:, :], up_scale).then_inc(scales_in.sem, 16)
                sp.dma_start(dsc[:, :], down_scale.partition_broadcast(P)).then_inc(scales_in.sem, 16)
                with sp.Fori(0, NQ - 1) as g:
                    load(1, "b", g, w_b, W_B, I32)
                    load(0, "b", g + 1, w_b, W_B, I32)
                load(1, "b", NQ - 1, w_b, W_B, I32)
                load(0, "c", None, w_c, W_A)
                load(1, "c", None, w_c, W_A)
                sp.wait_ge(resid.sem, resid.at("b", b, None, NT))
                sp.dma_start(rope1[:, :, :, :].rearrange("p a t d -> p (a t d)"), rope1_tables).then_inc(consts1_in.sem, 16)
                sp.dma_start(mask[:, :], causal).then_inc(consts1_in.sem, 16)
                sp.dma_start(ident_b[:, :], identity_b).then_inc(consts1_in.sem, 16)
                sp.dma_start(gate_bias[:, :], gate_b.partition_broadcast(P)).then_inc(consts1_in.sem, 16)
                sp.wait_ge(w_lo[0].sem, w_lo[0].at("d", b, None, 0))
                sp.dma_start(w_raw[:, 0:KD * D], w_gate).then_inc(w_in[0].sem, 16)
                for g in range(KV1):
                    sp.wait_ge(maxT_done.sem, maxT_done.at("c", b, None, g + 1))
                    for q in range(2):
                        sp.dma_start(QT[64 * q + ROW_M:64 * q + ROW_M + 1, 2 * g:2 * g + 2, :].bitcast(F32),
                                     maxT[2 * q:2 * q + 2, g % 2, :].bitcast(F32)).then_inc(m_in.sem, 16)
                sp.wait_ge(resid.sem, resid.at("c", b, None, NT))
                sp.dma_start(x3_dram[bass.ds(b, 1), :, :].rearrange("a (t p) d -> p (a t) d", p=P), X[:, :, :])\
                    .then_inc(x3_stored.sem, 16)
            sp.wait_ge(x3_stored.sem, 16 * (NB + 1))
            sp.wait_ge(gate_stored.sem, 16 * (NB + 1))

            sp.wait_ge(s_rows_clear, 1)
            sp.dma_start(rows[0:NB, :], x3_dram[:, S - 1, :]).then_inc(row_in, 16)
            sp.dma_start(aggw, agg_w).then_inc(row_in, 16)
            for n, c in enumerate((in_gamma, in_beta, agg_b, pn_gamma, pn_beta, d2_b, bc_b)):
                sp.dma_start(row_consts[:, n, :], c.partition_broadcast(R)).then_inc(row_in, 16)
            for n in range(4):
                sp.dma_start(bias1[32 * n:32 * n + 32, :], d1_b[n * D:(n + 1) * D].partition_broadcast(32)).then_inc(row_in, 16)
            sp.dma_start(summing[:, :], row_sum).then_inc(row_in, 16)
            sp.dma_start(d1w[:, :, :], d1_w).then_inc(row_in, 16)
            sp.dma_start(d2w[:, :, :], d2_w).then_inc(row_in, 16)
            sp.dma_start(bcw, bc_w).then_inc(row_in, 16)
            sp.dma_start(gam[:, :], out_gamma.partition_broadcast(P)).then_inc(d_in, 16)
            sp.dma_start(bet[:, :], out_beta.partition_broadcast(P)).then_inc(d_in, 16)
            sp.wait_ge(row.sem, row.at("post", 0, None, 2))
            sp.dma_start(bc_dram, rows[0:NB, :]).then_inc(s_bc_out, 16)
            sp.wait_ge(s_bc_out, 16)
            with sp.Fori(0, NB // 2) as pair:
                for s_ in range(2):
                    b = pair * 2 + s_
                    for t in range(NT):
                        sp.wait_ge(out_stored[s_][t].sem, out_stored[s_][t].at("o", pair, None, 0))
                        for dst, src in ((X_[s_], x3_dram), (G_[s_], gate_dram)):
                            sp.dma_start(dst[:, t, :], src[bass.ds(b, 1), t * P:(t + 1) * P, :].rearrange("a p d -> p (a d)"))\
                                .then_inc(x3_in[s_][t].sem, 16)
                    sp.dma_start(bcast[:, s_, :], bc_dram[bass.ds(b, 1), :].rearrange("a d -> (a d)").partition_broadcast(P))\
                        .then_inc(bc_in[s_].sem, 16)
            for s_ in range(2):
                for t in range(NT):
                    sp.wait_ge(out_stored[s_][t].sem, 16 * (NB // 2 + 1))

        def move_pack(copy, t, u):
            src = score_ps[u % 2][:, :].rearrange("p (n i) -> p n i", i=P)
            dst = QT[:, 4 * u:4 * u + 4, t * P:(t + 1) * P] if u < 4 else KT[:, 4 * (u - 4):4 * (u - 3), t * P:(t + 1) * P]
            return copy(dst, src)

        @block.gpsimd
        def _(pool):
            pool.memset(eps[:, :], LN_EPS).then_inc(s_pool_const, 1)
            pool.memset(minus_half[:, :], -0.5).then_inc(s_pool_const, 1)
            pool.wait_ge(s_pool_const, 2)
            pool.sem_inc(sin_done.sem, 1)

            def rstds(b, n):
                pool.wait_ge(ln_moments.sem, ln_moments.at("ln", b, None, n + 1))
                pool.tensor_tensor(var_eps[:, n:n + 1], moments[:, n, 1:2], eps[:, :], ALU.add)\
                    .then_inc(ln_var.sem, 1)
                pool.wait_ge(ln_var.sem, ln_var.at("ln", b, None, n + 1))
                pool.tensor_tensor(rstd[:, n:n + 1], var_eps[:, n:n + 1], minus_half[:, :], ALU.pow)\
                    .then_inc(ln_rstd.sem, 1)

            def handover(b, base, k):
                if k < 2 * NT:
                    rstds(b, base + k)
                if k >= 1 and HANDOVER[k - 1][0] == "post":
                    t = HANDOVER[k - 1][1]
                    pool.wait_ge(ln_out.sem, ln_out.at("ln", b, None, base + k))
                    pool.tensor_tensor(X[:, t, :], X[:, t, :], y_acc[:, t, :], ALU.add).then_inc(resid.sem, 1)

            with pool.Fori(0, NB) as b:
                for t in range(NT):
                    rstds(b, t)
                pool.wait_ge(gate_stored.sem, gate_stored.at("x", b, None, 0))
                pool.sem_inc(s_carry, 1)
                pool.memset(y_acc[:, :, :], 0.0).then_inc(cleared.sem, 1)
                def a_step(g, last):
                    pool.wait_ge(tables_in.sem, tables_in.at("a", b, None, 32))
                    for u in range(NU):
                        pool.wait_ge(rope_sum.sem, rope_sum.at("a", b, g, max(u - 1, 0)))
                        pool.wait_ge(swap_done.sem, swap_done.at("a", b, g, 2 * u + 2))
                        pool.tensor_tensor(sines[:, u % 2, :], swapped[:, u % 2, :], sinT[:, :], ALU.mult)\
                            .then_inc(sin_done.sem, 1)
                    for n in range(NBLK):
                        pool.wait_ge(p_hi.sem, p_hi.at("a", b, g, n + 1))
                        pool.tensor_tensor(pT[1][:, n % 4, :], pf[:, n % 2, :], pT[0][:, n % 4, :].bitcast(F32),
                                           ALU.subtract).then_inc(p_lo.sem, 1)
                        if last and n == WO_AFTER_BLOCK[0] + LAG:
                            handover(b, NT, 0)

                with pool.Fori(0, KV0 - 1) as g:
                    a_step(g, False)
                a_step(KV0 - 1, True)
                for k in range(1, 2 * NT):
                    handover(b, NT, k)
                pool.wait_ge(resid.sem, resid.at("a", b, None, NT))
                pool.sem_inc(s_carry, 1)
                pool.memset(y_acc[:, :, :], 0.0).then_inc(cleared.sem, 1)
                with pool.Fori(0, NQ) as g:
                    for m in range(IC):
                        pool.wait_ge(h_hi.sem, h_hi.at("b", b, g, m + 1))
                        pool.tensor_tensor(hT[1][:, m, :], hf[:, m % 2, :], hT[0][:, m, :].bitcast(F32),
                                           ALU.subtract).then_inc(h_lo.sem, 1)
                for k in range(2 * NT):
                    handover(b, 3 * NT, k)
                pool.wait_ge(resid.sem, resid.at("b", b, None, 1))
                pool.sem_inc(s_carry, 1)
                pool.memset(q_pack[:, :, ROW_M:64].bitcast(F32), 0.0).then_inc(pads.sem, 1)
                pool.memset(k_pack[:, :, :, ROW_M:ROW_M + 1].bitcast(F32), -1.0).then_inc(pads.sem, 1)
                pool.memset(k_pack[:, :, :, ROW_M + 1:64].bitcast(F32), 0.0).then_inc(pads.sem, 1)
                pool.memset(V1[:, :, :, HD1:HD1 + 1], 1.0).then_inc(pads.sem, 1)
                pool.memset(V1[:, :, :, HD1 + 1:32], 0.0).then_inc(pads.sem, 1)
                for g in range(KV1):
                    for j in range(NT):
                        pool.wait_ge(proj_free.sem, proj_free.at("s2", b, None, g * NS + S2_END[j]))
                        pool.sem_inc(s_carry, 1)
                        pool.affine_select(out=probs[j][:, :, 0:P], in_=probs[j][:, :, 0:P], compare_op=ALU.is_ge,
                                           fill=0.0, base=0, pattern=[[0, 4], [1, P]], channel_multiplier=-1)\
                            .then_inc(masked.sem, 1)
                for k in range(2 * NT):
                    handover(b, 5 * NT, k)

            def row_rstds(stage, g, k, eps_):
                pool.wait_ge(row.sem, row.at(stage, 0, g, 3 * k + 2))
                pool.tensor_tensor(var_eps[0:R, 0:1], moments[0:R, 0, 1:2], eps_[0:R, :], ALU.add).then_inc(row_var.sem, 1)
                pool.wait_ge(row_var.sem, row_var.at(stage, 0, g, k + 1))
                pool.tensor_tensor(rstd[0:R, 0:1], var_eps[0:R, 0:1], minus_half[0:R, :], ALU.pow).then_inc(row_rstd.sem, 1)

            pool.wait_ge(gate_stored.sem, 16 * (NB + 1))
            pool.memset(eps_ffn[:, :], EPS_FFN).then_inc(s_eps2, 1)
            pool.memset(rows[:, :], 0.0).then_inc(s_rows_clear, 1)
            pool.wait_ge(s_eps2, 1)
            row_rstds("pre", None, 0, eps)
            row_rstds("pre", None, 1, eps_ffn)
            with pool.Fori(0, K_STEPS) as g:
                row_rstds("step", g, 0, eps_ffn)
            with pool.Fori(0, NB // 2) as pair:
                for s_ in range(2):
                    b = pair * 2 + s_
                    for k, (at, eps_) in enumerate(((1, eps), (5, eps_ffn), (9, eps))):
                        for t in range(NT):
                            n = k * NT + t
                            pool.wait_ge(fin_step.sem, fin_step.at("o", b, None, at * NT + t + 1))
                            pool.tensor_tensor(var_eps[:, n:n + 1], moments[:, n, 1:2], eps_[:, :], ALU.add)\
                                .then_inc(fin_var.sem, 1)
                            pool.wait_ge(fin_var.sem, fin_var.at("o", b, None, n + 1))
                            pool.tensor_tensor(rstd[:, n:n + 1], var_eps[:, n:n + 1], minus_half[:, :], ALU.pow)\
                                .then_inc(fin_rstd.sem, 1)
                        if k == 0:
                            pool.wait_ge(bc_in[s_].sem, bc_in[s_].at("o", pair, None, 16))
                            for t in range(NT):
                                gate = G_[s_][:, t, :]
                                pool.tensor_tensor(gate, gate, bcast[:, s_, :], ALU.mult).then_inc(fin_gate.sem, 1)
                    for t in range(NT):
                        pool.wait_ge(fin_step.sem, fin_step.at("o", b, None, 10 * NT + t + 1))
                        z = Z_[s_][:, t, :]
                        pool.tensor_tensor(z, z, X_[s_][:, t, :], ALU.add).then_inc(fin_out.sem, 1)

        @block.scalar
        def _(act):
            def copy(out_, in_):
                return act.activation(out_, in_, ACT.Copy)

            def front(stage, b):
                for t in range(NT):
                    act.wait_ge(proj.sem, proj.at("front_" + stage, b, None, t + 1))
                    copy(XnT[0][:, :, t * P:(t + 1) * P],
                         proj_ps[t % 2][:, :].rearrange("p (k i) -> p k i", k=KD)).then_inc(front_hi.sem, 1)

            act.sem_inc(moved[0].sem, 1)
            act.sem_inc(gate_stored.sem, 16)
            for s_ in range(2):
                for t in range(NT):
                    act.sem_inc(out_stored[s_][t].sem, 16)
            with act.Fori(0, NB) as b:
                def split(n, stage, g, c):
                    if c == 0:
                        act.wait_ge(w_in[n].sem, w_in[n].at(stage, b, g, 16))
                    src, bias = (chunk(w_raw, n, c).bitcast(I32), -ZERO_POINT) if stage == "b" else (chunk(w_raw, n, c), 0.0)
                    act.activation(chunk(W[0], n, c), src, ACT.Copy, bias=bias).then_inc(w_hi[n].sem, 1)

                for c in range(CHUNKS[0]["a"]):
                    split(0, "a", 0, c)
                front("a", b)

                def a_step(g, following):
                    def swap(u):
                        act.wait_ge(sin_done.sem, sin_done.at("a", b, g, max(u - 1, 0)))
                        act.wait_ge(proj.sem, proj.at("a", b, g, u + 1))
                        half = P // 2
                        ps = proj_ps[u % 2]
                        copy(swapped[0:half, u % 2, :], ps[half:P, :]).then_inc(swap_done.sem, 1)
                        copy(swapped[half:P, u % 2, :], ps[0:half, :]).then_inc(swap_done.sem, 1)

                    def rope_high(u):
                        act.wait_ge(rope_sum.sem, rope_sum.at("a", b, g, u + 1))
                        dst = kT[0][:, :] if u == 0 else qT[0][:, u - 1, :]
                        copy(dst, roped[:, u % 3, :]).then_inc(rope_hi.sem, 1)

                    act.wait_ge(y.sem, y.at("a", b, g, 0))
                    for c in range(CHUNKS[1]["a"]):
                        split(1, "a", g, c)
                    swap(0)
                    for u in range(1, NU):
                        swap(u)
                        rope_high(u - 1)
                    rope_high(NU - 1)
                    for n in range(NBLK + LAG):
                        if n < NBLK:
                            act.wait_ge(pv_done.sem, pv_done.at("a", b, g, n - 3))
                            act.wait_ge(p_f.sem, p_f.at("a", b, g, n + 1))
                            copy(pT[0][:, n % 4, :], pf[:, n % 2, :]).then_inc(p_hi.sem, 1)
                            if n < 2:
                                act.wait_ge(proj.sem, proj.at("a", b, g, NU + 2 + n))
                                copy(v[0][:, 2 * n:2 * n + 2, :],
                                     proj_ps[n][:, 0:2 * P].rearrange("p (t e) -> p t e", t=2)).then_inc(v_hi.sem, 1)
                        if n - LAG in LAST:
                            i = LAST.index(n - LAG)
                            act.wait_ge(pv_done.sem, pv_done.at("a", b, g, n - LAG + 1))
                            copy(oT[0][:, :, i * P:(i + 1) * P], o_ps[i % 2][:, :].rearrange("p (h i) -> p h i", h=HG))\
                                .then_inc(o_hi.sem, 1)
                        if SPLIT_AT.get(n, 4) < CHUNKS[0][following[0]]:
                            split(0, *following, SPLIT_AT[n])

                with act.Fori(0, KV0 - 1) as g:
                    a_step(g, ("a", g + 1))
                a_step(KV0 - 1, ("b", 0))
                front("b", b)

                def b_step(g, following):
                    act.wait_ge(scales_in.sem, scales_in.at("b", b, None, 48))
                    act.wait_ge(y.sem, y.at("b", b, g, 0))
                    for m in range(IC):
                        act.wait_ge(h_f.sem, h_f.at("b", b, g, m - 1))
                        act.wait_ge(proj.sem, proj.at("b", b, g, m + 1))
                        act.activation(silu[:, m % 2, :], proj_ps[m % 2][:, :], ACT.Silu,
                                       scale=gsc[:, bass.ds(g * IC + m, 1)]).then_inc(proj_free.sem, 1)
                        if m >= 1:
                            act.wait_ge(h_f.sem, h_f.at("b", b, g, m))
                            copy(hT[0][:, m - 1, :], hf[:, (m - 1) % 2, :]).then_inc(h_hi.sem, 1)
                        if m < CHUNKS[1]["b"]:
                            split(1, "b", g, m)
                    act.wait_ge(h_f.sem, h_f.at("b", b, g, IC))
                    copy(hT[0][:, IC - 1, :], hf[:, (IC - 1) % 2, :]).then_inc(h_hi.sem, 1)
                    for c in range(CHUNKS[0][following[0]]):
                        split(0, *following, c)

                with act.Fori(0, NQ - 1) as g:
                    b_step(g, ("b", g + 1))
                b_step(NQ - 1, ("c", None))
                front("c", b)

                def moves(t):
                    for u in (0, 2, 4):
                        act.wait_ge(score.sem, score.at("pack", b, None, 6 * t + u + 1))
                        move_pack(copy, t, u).then_inc(moved[0].sem, 1)

                for t in range(NT):
                    if t >= 1:
                        moves(t - 1)
                        act.wait_ge(score.sem, score.at("pack", b, None, 6 * t))
                    else:
                        act.wait_ge(pads.sem, pads.at("c", b, None, 5))
                    q_, k_ = ra[:, 0:NR].rearrange("p (h d) -> p h d", h=H1), ra[:, NR:].rearrange("p (h d) -> p h d", h=KV1)
                    act.wait_ge(rot_sum.sem, rot_sum.at("c", b, None, 2 * t + 1))
                    for n in range(2):
                        copy(q_pack[:, :, n * HD1:(n + 1) * HD1], q_).then_inc(rot_hi.sem, 1)
                    act.wait_ge(rot_sum.sem, rot_sum.at("c", b, None, 2 * t + 2))
                    for n in range(2):
                        copy(k_pack[:, :, :, 2 * n * HD1:(2 * n + 1) * HD1],
                             k_.unsqueeze(2).to_broadcast([P, KV1, 2, HD1])).then_inc(rot_hi.sem, 1)
                moves(NT - 1)
                act.wait_ge(y.sem, y.at("c", b, None, 0))
                for c in range(CHUNKS[1]["c"]):
                    split(1, "c", None, c)
                for c in range(CHUNKS[0]["d"]):
                    split(0, "d", None, c)
                for g in range(KV1):
                    for u, (j, heads) in enumerate(S2_BANKS):
                        n = g * NS + u
                        if u == 0 or S2_BANKS[u - 1][0] != j:
                            act.wait_ge(pv1.sem, pv1.at("c", b, None, (g - 1) * NT + j + 1))
                        act.wait_ge(proj.sem, proj.at("s2", b, None, n + 1))
                        h0, w = HEADS1.index(heads[0]), S - j * P
                        act.activation(probs[j][:, h0:h0 + len(heads), :],
                                       proj_ps[n % 2][:, 0:len(heads) * w].rearrange("p (h i) -> p h i", i=w), ACT.Exp)\
                            .then_inc(proj_free.sem, 1)
                front("y", b)
                front("d", b)
                for t in range(NT):
                    act.wait_ge(y_free.sem, y_free.at("d", b, None, t + 1))
                    act.activation(y_acc[:, t, :], y_acc[:, t, :], ACT.Sigmoid).then_inc(gate_done.sem, 1)
                act.wait_ge(gate_done.sem, gate_done.at("d", b, None, NT))
                act.dma_start(gate_dram[bass.ds(b, 1), :, :].rearrange("a (t p) d -> p (a t) d", p=P), y_acc[:, :, :])\
                    .then_inc(gate_stored.sem, 16)

            with act.Fori(0, K_STEPS) as g:
                act.wait_ge(row.sem, row.at("step", 0, g, 7))
                act.activation(hidden, hidden, ACT.Gelu).then_inc(gelu_done.sem, 1)
            with act.Fori(0, NB // 2) as pair:
                for s_ in range(2):
                    b = pair * 2 + s_
                    for t in range(NT):
                        act.wait_ge(fin_out.sem, fin_out.at("o", b, None, t + 1))
                        act.dma_start(out[bass.ds(b, 1), t * P:(t + 1) * P, :].rearrange("a p d -> p (a d)"), Z_[s_][:, t, :])\
                            .then_inc(out_stored[s_][t].sem, 16)

        @block.vector
        def _(dve):
            for free in (ln_out, proj_free, o_free, y_free, rope_sum, p_f, h_f):
                dve.sem_inc(free.sem, free.credit)
            for n in range(2):
                dve.sem_inc(w_lo[n].sem, 1)
            dve.sem_inc(p_lo.sem, 2)
            dve.sem_inc(rope_lo.sem, 1)
            dve.sem_inc(h_lo.sem, 2)
            for free in (rot_sum, rot_lo, moved[1], s_max, yT_done, y1_done):
                dve.sem_inc(free.sem, free.credit)

            def measure(b, n, src):
                dve.bn_stats(stats[:, n, :], src).then_inc(ln_stats.sem, 1)
                dve.wait_ge(ln_stats.sem, ln_stats.at("ln", b, None, n + 1))
                dve.sem_inc(s_carry, 1)
                dve.bn_aggr(moments[:, n, :], stats[:, n, :]).then_inc(ln_moments.sem, 1)

            def norm(b, n, dst, src):
                dve.wait_ge(ln_rstd.sem, ln_rstd.at("ln", b, None, n + 1))
                dve.tensor_scalar(dst, src, moments[:, n, 0:1], rstd[:, n:n + 1], ALU.subtract, ALU.mult)\
                    .then_inc(ln_out.sem, 1)

            def low(dst, full, high):
                return dve.tensor_tensor(dst, full, high.bitcast(F32), ALU.subtract)

            def front_low(stage, b, t):
                dve.wait_ge(front_hi.sem, front_hi.at(stage, b, None, t + 1))
                low(XnT[1][:, :, t * P:(t + 1) * P], proj_ps[t % 2][:, :].rearrange("p (k i) -> p k i", k=KD),
                    XnT[0][:, :, t * P:(t + 1) * P]).then_inc(proj_free.sem, 1)

            def handover(stage, following, base, b, k):
                if k < 2 * NT:
                    which, t = HANDOVER[k]
                    if which == "pre":
                        dve.wait_ge(resid.sem, resid.at(stage, b, None, t + 1))
                    measure(b, base + k, y_acc[:, t, :] if which == "post" else X[:, t, :])
                if k >= 1:
                    which, t = HANDOVER[k - 1]
                    n = base + k - 1
                    if which == "post":
                        norm(b, n, y_acc[:, t, :], y_acc[:, t, :])
                    else:
                        if t >= 2:
                            front_low(following, b, t - 2)
                        norm(b, n, xn[:, t % 2, :], X[:, t, :])

            HANDOVER_AT = {0: (0,), 1: (1,), 2: (2, 3), 3: (4, 5, 6, 7, 8)}

            def split(n, stage, b, g, c):
                dve.wait_ge(w_hi[n].sem, w_hi[n].at(stage, b, g, c + 1))
                if stage == "b":
                    last = dve.scalar_tensor_tensor(chunk(W[1], n, c), chunk(w_raw, n, c).bitcast(I32), -ZERO_POINT,
                                                    chunk(W[0], n, c).bitcast(F32), ALU.add, ALU.subtract)
                else:
                    last = low(chunk(W[1], n, c), chunk(w_raw, n, c), chunk(W[0], n, c))
                last.then_inc(w_lo[n].sem, 1)

            with dve.Fori(0, NB) as b:
                dve.wait_ge(x_in.sem, x_in.at("x", b, None, 16))
                for t in range(NT):
                    measure(b, t, X[:, t, :])
                for t in range(NT):
                    if t >= 2:
                        front_low("a", b, t - 2)
                    norm(b, t, xn[:, t % 2, :], X[:, t, :])
                    if 1 <= t <= CHUNKS[0]["a"]:
                        split(0, "a", b, 0, t - 1)
                for t in (NT - 2, NT - 1):
                    front_low("a", b, t)

                def a_step(g, following):
                    dve.wait_ge(tables_in.sem, tables_in.at("a", b, None, 32))

                    def cosine(u):
                        dve.wait_ge(rope_lo.sem, rope_lo.at("a", b, g, max(u - 2, 0)))
                        dve.wait_ge(swap_done.sem, swap_done.at("a", b, g, 2 * u + 2))
                        dve.tensor_tensor(roped[:, u % 3, :], proj_ps[u % 2][:, :], cosT[:, :], ALU.mult)\
                            .then_inc(proj_free.sem, 1)

                    def rotate(u):
                        dve.wait_ge(proj_free.sem, proj_free.at("a", b, g, u + 1))
                        dve.wait_ge(sin_done.sem, sin_done.at("a", b, g, u + 1))
                        dve.tensor_tensor(roped[:, u % 3, :], roped[:, u % 3, :], sines[:, u % 2, :], ALU.add)\
                            .then_inc(rope_sum.sem, 1)

                    def rope_low(u):
                        dve.wait_ge(rope_hi.sem, rope_hi.at("a", b, g, u + 1))
                        dst, high = (kT[1][:, :], kT[0][:, :]) if u == 0 else (qT[1][:, u - 1, :], qT[0][:, u - 1, :])
                        low(dst, roped[:, u % 3, :], high).then_inc(rope_lo.sem, 1)

                    for c in range(CHUNKS[1]["a"]):
                        split(1, "a", b, g, c)
                    cosine(0)
                    for u in range(1, NU):
                        cosine(u)
                        rotate(u - 1)
                        if u >= 2:
                            rope_low(u - 2)
                    rotate(NU - 1)
                    rope_low(NU - 2)
                    rope_low(NU - 1)
                    dve.wait_ge(proj.sem, proj.at("a", b, g, NU + 1))
                    dve.tensor_copy(vT[:, :], proj_ps[NU % 2][:, :]).then_inc(proj_free.sem, 1)
                    dve.wait_ge(decay_in.sem, decay_in.at("a", b, g, 16))

                    def accumulate(t):
                        dve.wait_ge(y.sem, y.at("a", b, g, t + 1))
                        dve.tensor_tensor(y_acc[:, t, :], y_ps[t % 2][:, :], y_acc[:, t, :], ALU.add)\
                            .then_inc(y_free.sem, 1)
                        if following[0] == "b":
                            dve.wait_ge(y_free.sem, y_free.at("a", b, g, t + 1))
                            for k in HANDOVER_AT[t]:
                                handover("a", "b", NT, b, k)

                    dve.wait_ge(cleared.sem, cleared.at("a", b, None, 1))
                    dve.wait_ge(y_free.sem, y_free.at("a", b, g, 0))
                    for n in range(NBLK + LAG + 1):
                        if n < NBLK:
                            i, j = BLOCKS[n]
                            dve.wait_ge(p_lo.sem, p_lo.at("a", b, g, n - 1))
                            dve.wait_ge(score.sem, score.at("a", b, g, n + 1))
                            dve.tensor_tensor(pf[:, n % 2, :].rearrange("p (h i) -> p h i", h=HG),
                                              score_ps[n % 2][:, :].rearrange("p (h i) -> p h i", h=HG),
                                              dec[:, :, i - j, :], ALU.mult).then_inc(p_f.sem, 1)
                            if 1 <= n <= 2:
                                dve.wait_ge(v_hi.sem, v_hi.at("a", b, g, n))
                                low(v[1][:, 2 * n - 2:2 * n, :],
                                    proj_ps[n - 1][:, 0:2 * P].rearrange("p (t e) -> p t e", t=2),
                                    v[0][:, 2 * n - 2:2 * n, :]).then_inc(proj_free.sem, 1)
                        if n - LAG - 1 in LAST:
                            i = LAST.index(n - LAG - 1)
                            dve.wait_ge(o_hi.sem, o_hi.at("a", b, g, i + 1))
                            low(oT[1][:, :, i * P:(i + 1) * P], o_ps[i % 2][:, :].rearrange("p (h i) -> p h i", h=HG),
                                oT[0][:, :, i * P:(i + 1) * P]).then_inc(o_free.sem, 1)
                        if SPLIT_AT.get(n - 1, 4) < CHUNKS[0][following[0]]:
                            split(0, following[0], b, following[1], SPLIT_AT[n - 1])
                        if n < NBLK + LAG:
                            for t in WO_AFTER.get(n - LAG - 1, []):
                                accumulate(t)
                    for t in WO_AFTER[NBLK - 1]:
                        accumulate(t)

                with dve.Fori(0, KV0 - 1) as g:
                    a_step(g, ("a", g + 1))
                a_step(KV0 - 1, ("b", 0))
                for t in (NT - 2, NT - 1):
                    front_low("b", b, t)

                def b_step(g, following):
                    dve.wait_ge(scales_in.sem, scales_in.at("b", b, None, 48))
                    dve.wait_ge(cleared.sem, cleared.at("b", b, None, 1))
                    for m in range(IC):
                        dve.wait_ge(h_lo.sem, h_lo.at("b", b, g, m - 1))
                        dve.wait_ge(score.sem, score.at("b", b, g, m + 1))
                        dve.wait_ge(proj_free.sem, proj_free.at("b", b, g, m + 1))
                        dve.scalar_tensor_tensor(hf[:, m % 2, :], score_ps[m % 2][:, :], usc[:, bass.ds(g * IC + m, 1)],
                                                 silu[:, m % 2, :], ALU.mult, ALU.mult).then_inc(h_f.sem, 1)
                        if m < CHUNKS[1]["b"]:
                            split(1, "b", b, g, m)
                    dve.wait_ge(y_free.sem, y_free.at("b", b, g, 0))
                    for t in range(NT):
                        for c in ((0, 1), (2,), (3,), ())[t]:
                            if c < CHUNKS[0][following[0]]:
                                split(0, following[0], b, following[1], c)
                        dve.wait_ge(y.sem, y.at("b", b, g, t + 1))
                        dve.tensor_tensor(y_acc[:, t, :], y_ps[t % 2][:, :], y_acc[:, t, :], ALU.add)\
                            .then_inc(y_free.sem, 1)
                        if following[0] == "c":
                            dve.wait_ge(y_free.sem, y_free.at("b", b, g, t + 1))
                            dve.tensor_tensor(y_acc[:, t, :], y_acc[:, t, :], dsc[:, :], ALU.mult).then_inc(y_scaled.sem, 1)
                            dve.wait_ge(y_scaled.sem, y_scaled.at("b", b, None, t + 1))
                            for k in HANDOVER_AT[t]:
                                handover("b", "c", 3 * NT, b, k)

                with dve.Fori(0, NQ - 1) as g:
                    b_step(g, ("b", g + 1))
                b_step(NQ - 1, ("c", None))
                for t in (NT - 2, NT - 1):
                    front_low("c", b, t)
                dve.wait_ge(consts1_in.sem, consts1_in.at("c", b, None, 64))
                dve.wait_ge(pads.sem, pads.at("c", b, None, 5))

                def moves(t):
                    for u in (1, 3, 5):
                        dve.wait_ge(score.sem, score.at("pack", b, None, 6 * t + u + 1))
                        move_pack(dve.tensor_copy, t, u).then_inc(moved[1].sem, 1)

                def rotate_pairs(t, part, ps, lo_, nh):
                    cos_, sin_ = rope1[:, 2 * part, t, :], rope1[:, 2 * part + 1, t, :]
                    w = nh * HD1
                    a_, b_ = ra[:, lo_:lo_ + w], rb[:, lo_:lo_ + w]
                    dve.wait_ge(proj.sem, proj.at("qkv", b, None, 2 * t + part + 1))
                    dve.wait_ge(rot_lo.sem, rot_lo.at("c", b, None, 2 * t))
                    dve.wait_ge(rot_sum.sem, rot_sum.at("c", b, None, 2 * t))
                    dve.tensor_tensor(a_.rearrange("p (h d) -> p h d", h=nh), ps[:, 0:w].rearrange("p (h d) -> p h d", h=nh),
                                      cos_.unsqueeze(1).to_broadcast([P, nh, HD1]), ALU.mult)
                    pairs = [z.rearrange("p (h d two) -> p h d two", h=nh, two=2) for z in (b_, ps[:, 0:w])]
                    s2_ = sin_.rearrange("p (d two) -> p d two", two=2)
                    for e in range(2):
                        last = dve.tensor_tensor(pairs[0][:, :, :, e], pairs[1][:, :, :, 1 - e],
                                                 s2_[:, :, e].unsqueeze(1).to_broadcast([P, nh, HD1 // 2]), ALU.mult)
                        if e == 0:
                            continue
                        last.then_inc(proj_free.sem, 1) if part == 0 else last.then_inc(rot_k.sem, 1)
                    if part == 1:
                        dve.wait_ge(rot_k.sem, rot_k.at("c", b, None, t + 1))
                        dve.tensor_copy(V1[:, t, :, 0:HD1], ps[:, w:2 * w].rearrange("p (h d) -> p h d", h=nh))\
                            .then_inc(proj_free.sem, 1)
                    else:
                        dve.wait_ge(proj_free.sem, proj_free.at("qkv", b, None, 2 * t + 1))
                    dve.tensor_tensor(a_, a_, b_, ALU.add).then_inc(rot_sum.sem, 1)

                for t in range(NT):
                    rotate_pairs(t, 0, proj_ps[0], 0, H1)
                    rotate_pairs(t, 1, proj_ps[1], NR, KV1)
                    if t >= 1:
                        moves(t - 1)
                    q_, k_ = ra[:, 0:NR].rearrange("p (h d) -> p h d", h=H1), ra[:, NR:].rearrange("p (h d) -> p h d", h=KV1)
                    dve.wait_ge(rot_hi.sem, rot_hi.at("c", b, None, 4 * t + 2))
                    low(q_pack[:, :, 2 * HD1:3 * HD1], q_, q_pack[:, :, 0:HD1]).then_inc(rot_lo.sem, 1)
                    dve.wait_ge(rot_hi.sem, rot_hi.at("c", b, None, 4 * t + 4))
                    low(k_pack[:, :, :, HD1:2 * HD1], k_.unsqueeze(2).to_broadcast([P, KV1, 2, HD1]),
                        k_pack[:, :, :, 0:HD1]).then_inc(rot_lo.sem, 1)
                moves(NT - 1)
                for k in range(KV1 + 3):
                    for u in range(NS):
                        if k < KV1:
                            i, heads = S1_BANKS[u]
                            (q, n), w = heads[0], (i + 1) * P
                            dst = row_max[:, k, i, q, n:n + len(heads)]
                            src = score_ps[(k * NS + u) % 2][:, 0:len(heads) * w].rearrange("p (n s) -> p n s", s=w)
                            dve.wait_ge(score.sem, score.at("s1", b, None, k * NS + u + 1))
                            dve.reduce_max(dst, src, AX_X).then_inc(s_max.sem, 1)
                        if k < 2 and u in (4, 8):
                            split(1 - k, "cd"[k], b, None, u // 4 - 1)
                        g = k - 1
                        if u == 2 and 0 <= g < KV1:
                            dve.wait_ge(m_in.sem, m_in.at("c", b, None, 32 * max(g - 1, 0)))
                            dve.wait_ge(max_rows.sem, max_rows.at("c", b, None, g + 1))
                            dve.tensor_copy(maxT[:, g % 2, :], y_ps[0][0:4, :]).then_inc(maxT_done.sem, 1)
                        g = k - 3
                        if g >= 0 and u == 3:
                            dve.wait_ge(pv1.sem, pv1.at("c", b, None, (g + 1) * NT))
                            dve.tensor_copy(yT[:, g % 2, :], o_ps[g % 2][:, :]).then_inc(yT_done.sem, 1)
                        if g >= 0 and u == 8:
                            ps = y_ps[1][:, :].rearrange("p (i h d) -> p (i h) d", h=4, d=32)
                            dve.wait_ge(y_back.sem, y_back.at("c", b, None, g + 1))
                            dve.wait_ge(y1_done.sem, y1_done.at("c", b, None, g - 1))
                            dve.reciprocal(rden[:, g % 2, :], ps[:, :, HD1:HD1 + 1].rearrange("p n a -> p (n a)")).then_inc(den_done.sem, 1)
                            dve.wait_ge(den_done.sem, den_done.at("c", b, None, g + 1))
                            dve.tensor_tensor(y_acc[:, :, g * 4 * HD1:(g + 1) * 4 * HD1].rearrange("p i (h d) -> p i h d", h=4),
                                              ps[:, :, 0:HD1].rearrange("p (i h) d -> p i h d", h=4),
                                              rden[:, g % 2, :].rearrange("p (i h) -> p i h", h=4).unsqueeze(3)
                                              .to_broadcast([P, NT, 4, HD1]), ALU.mult).then_inc(y1_done.sem, 1)
                for t in range(NT):
                    front_low("y", b, t)
                for t in range(NT):
                    dve.wait_ge(y.sem, y.at("c", b, None, t + 1))
                    dve.tensor_copy(y_acc[:, t, :], y_ps[t % 2][:, :]).then_inc(y_free.sem, 1)
                    dve.wait_ge(y_free.sem, y_free.at("c", b, None, t + 1))
                    for k in HANDOVER_AT[t]:
                        handover("c", "d", 5 * NT, b, k)
                for t in (NT - 2, NT - 1):
                    front_low("d", b, t)
                for t in range(NT):
                    dve.wait_ge(y.sem, y.at("d", b, None, t + 1))
                    dve.tensor_tensor(y_acc[:, t, :], y_ps[t % 2][:, :], gate_bias[:, :], ALU.add).then_inc(y_free.sem, 1)

            def row_norm(stage, g, k, m, dst, src):
                dve.bn_stats(stats[0:R, 0, :], src).then_inc(row.sem, 1)
                dve.wait_ge(row.sem, row.at(stage, 0, g, k + 1))
                dve.sem_inc(s_carry, 1)
                dve.bn_aggr(moments[0:R, 0, :], stats[0:R, 0, :]).then_inc(row.sem, 1)
                dve.wait_ge(row_rstd.sem, row_rstd.at(stage, 0, g, m + 1))
                dve.tensor_scalar(dst, src, moments[0:R, 0, 0:1], rstd[0:R, 0:1], ALU.subtract, ALU.mult).then_inc(row.sem, 1)
                dve.wait_ge(row.sem, row.at(stage, 0, g, k + 3))

            def row_affine(stage, g, k, n):
                dve.tensor_tensor(rows[:, :], rows[:, :], row_consts[:, n, :], ALU.mult).then_inc(row.sem, 1)
                dve.wait_ge(row.sem, row.at(stage, 0, g, k + 1))
                dve.tensor_tensor(rows[:, :], rows[:, :], row_consts[:, n + 1, :], ALU.add).then_inc(row.sem, 1)

            def rows_T(stage, g, mm):
                dve.wait_ge(row_mm.sem, row_mm.at(stage, 0, g, mm))
                dve.tensor_copy(rowsT[:, :, :].rearrange("p c r -> p (c r)"), o_ps[0][:, 0:KD * R]).then_inc(row.sem, 1)

            dve.wait_ge(row_in, ROW_INS)
            row_norm("pre", None, 0, 0, rows[:, :], rows[:, :])
            row_norm("pre", None, 3, 1, rows[:, :], rows[:, :])
            row_affine("pre", None, 6, 0)
            rows_T("pre", None, 1)
            dve.wait_ge(row_mm.sem, row_mm.at("pre", 0, None, 2))
            dve.tensor_tensor(thought[:, :], o_ps[1][0:R, :], row_consts[:, 2, :], ALU.add).then_inc(row.sem, 1)
            with dve.Fori(0, K_STEPS) as g:
                dve.wait_ge(row.sem, row.at("step", 0, g, 0))
                row_norm("step", g, 0, 0, rows[:, :], thought[:, :])
                row_affine("step", g, 3, 3)
                rows_T("step", g, 1)
                dve.wait_ge(row_mm.sem, row_mm.at("step", 0, g, 2))
                dve.tensor_tensor(hidden, score_ps[0][:, :], bias1[:, :], ALU.add).then_inc(row.sem, 1)
                dve.wait_ge(row_mm.sem, row_mm.at("step", 0, g, 3))
                dve.tensor_copy(hiddenT[:, :, :].rearrange("p c r -> p (c r)"), score_ps[1][:, :]).then_inc(row.sem, 1)
                dve.wait_ge(row_mm.sem, row_mm.at("step", 0, g, 4))
                dve.tensor_copy(partial, proj_ps[0][:, :]).then_inc(row.sem, 1)
                dve.wait_ge(row_mm.sem, row_mm.at("step", 0, g, 5))
                dve.tensor_tensor(rows[:, :], proj_ps[1][0:R, :], row_consts[:, 5, :], ALU.add).then_inc(row.sem, 1)
                dve.wait_ge(row.sem, row.at("step", 0, g, 10))
                dve.tensor_tensor(thought[:, :], thought[:, :], rows[:, :], ALU.add).then_inc(row.sem, 1)
            rows_T("post", None, 1)
            dve.wait_ge(row_mm.sem, row_mm.at("post", 0, None, 2))
            dve.tensor_tensor(rows[:, :], o_ps[1][0:R, :], row_consts[:, 6, :], ALU.add).then_inc(row.sem, 1)

            dve.wait_ge(d_in, 32)
            with dve.Fori(0, NB // 2) as pair:
                for s_ in range(2):
                    b = pair * 2 + s_
                    X_b, G_b, Z_b = X_[s_], G_[s_], Z_[s_]

                    def done(k, t):
                        dve.wait_ge(fin_step.sem, fin_step.at("o", b, None, k * NT + t + 1))

                    def fin_measure(k, m, src, first):
                        for t in range(NT):
                            if first:
                                dve.wait_ge(x3_in[s_][t].sem, x3_in[s_][t].at("o", pair, None, 32))
                            else:
                                done(k - 1, t)
                            dve.bn_stats(stats[:, m * NT + t, :], src[:, t, :]).then_inc(fin_step.sem, 1)
                        for t in range(NT):
                            done(k, t)
                            dve.sem_inc(s_carry, 1)
                            dve.bn_aggr(moments[:, m * NT + t, :], stats[:, m * NT + t, :]).then_inc(fin_step.sem, 1)

                    def fin_norm(m, src):
                        for t in range(NT):
                            n = m * NT + t
                            dve.wait_ge(fin_rstd.sem, fin_rstd.at("o", b, None, n + 1))
                            dve.tensor_scalar(Z_b[:, t, :], src[:, t, :], moments[:, n, 0:1], rstd[:, n:n + 1],
                                              ALU.subtract, ALU.mult).then_inc(fin_step.sem, 1)

                    fin_measure(0, 0, X_b, True)
                    fin_norm(0, X_b)
                    for t in range(NT):
                        dve.wait_ge(fin_gate.sem, fin_gate.at("o", b, None, t + 1))
                        done(2, t)
                        dve.tensor_tensor(Z_b[:, t, :], Z_b[:, t, :], G_b[:, t, :], ALU.add).then_inc(fin_step.sem, 1)
                    fin_measure(4, 1, Z_b, False)
                    for t in range(NT):
                        n = NT + t
                        dve.wait_ge(fin_rstd.sem, fin_rstd.at("o", b, None, n + 1))
                        dve.scalar_tensor_tensor(Z_b[:, t, :], Z_b[:, t, :], moments[:, n, 0:1], gam[:, :],
                                                 ALU.subtract, ALU.mult).then_inc(fin_step.sem, 1)
                    for t in range(NT):
                        n = NT + t
                        done(6, t)
                        dve.scalar_tensor_tensor(Z_b[:, t, :], Z_b[:, t, :], rstd[:, n:n + 1], bet[:, :],
                                                 ALU.mult, ALU.add).then_inc(fin_step.sem, 1)
                    fin_measure(8, 2, Z_b, False)
                    fin_norm(2, Z_b)

        @block.tensor
        def _(pe):
            pe.sem_inc(y.sem, 1)
            pe.sem_inc(pv_done.sem, 4)
            pe.sem_inc(pv1.sem, 4)
            pe.wait_ge(s_ident, 16)

            def product(dst, terms, before=lambda n: None):
                n = 3 * len(terms)
                k = 0
                for at, (stat, mov) in enumerate(terms):
                    before(at)
                    for s_, m_ in ((0, 0), (1, 0), (0, 1)):
                        last = pe.matmul(dst, stat[s_], mov[m_], start=(k == 0), stop=(k == n - 1))
                        k += 1
                return last

            def front(stage, b):
                for t in range(NT):
                    pe.wait_ge(proj_free.sem, proj_free.at("front_" + stage, b, None, t - 1))
                    if stage == "y":
                        pe.wait_ge(y1_done.sem, y1_done.at("c", b, None, KV1))
                    else:
                        n = t if stage == "a" else {"b": NT, "c": 3 * NT, "d": 5 * NT}[stage] + HANDOVER.index(("pre", t))
                        pe.wait_ge(ln_out.sem, ln_out.at("ln", b, None, n + 1))
                    src = y_acc[:, t, :] if stage == "y" else xn[:, t % 2, :]
                    for c in range(KD):
                        last = pe.transpose(proj_ps[t % 2][:, c * P:(c + 1) * P], src[:, c * P:(c + 1) * P],
                                            ident[:, :])
                    last.then_inc(proj.sem, 1)

            with pe.Fori(0, NB) as b:
                front("a", b)
                with pe.Fori(0, KV0) as g:
                    pe.wait_ge(proj_free.sem, proj_free.at("a", b, g, 0))
                    pe.wait_ge(w_lo[0].sem, w_lo[0].at("a", b, g, CHUNKS[0]["a"]))

                    def project(use, w):
                        pe.wait_ge(proj_free.sem, proj_free.at("a", b, g, use - 1))
                        product(proj_ps[use % 2][:, :],
                                [([w(W[s_], c) for s_ in range(2)], [XnT[m_][:, c, :] for m_ in range(2)])
                                 for c in range(KD)]).then_inc(proj.sem, 1)

                    project(0, wk)
                    for h in range(HG):
                        project(1 + h, lambda t, c: wq(t, c, h))
                    project(NU, wv)
                    pe.wait_ge(rope_lo.sem, rope_lo.at("a", b, g, NU))

                    for n in range(NBLK + LAG):
                        if n < NBLK:
                            i, j = BLOCKS[n]
                            pe.wait_ge(p_f.sem, p_f.at("a", b, g, n - 1))
                            product(score_ps[n % 2][:, :].rearrange("p (h i) -> p h i", h=HG),
                                    [([kT[s_][:, j * P:(j + 1) * P] for s_ in range(2)],
                                      [qT[m_][:, :, i * P:(i + 1) * P] for m_ in range(2)])]).then_inc(score.sem, 1)
                        if n < 2:
                            pe.wait_ge(proj_free.sem, proj_free.at("a", b, g, NU + 1))
                            for t in range(2):
                                last = pe.transpose(proj_ps[n][:, t * P:(t + 1) * P], vT[:, (2 * n + t) * P:(2 * n + t + 1) * P],
                                                    ident[:, :])
                            last.then_inc(proj.sem, 1)
                        m = n - LAG
                        if m >= 0:
                            i, j = BLOCKS[m]
                            if m == 0:
                                pe.wait_ge(proj_free.sem, proj_free.at("a", b, g, PROJ_A))
                            if j == 0:
                                pe.wait_ge(o_free.sem, o_free.at("a", b, g, i - 1))
                            pe.wait_ge(p_lo.sem, p_lo.at("a", b, g, m + 1))
                            for k, (s_, m_) in enumerate(((0, 0), (1, 0), (0, 1))):
                                last = pe.matmul(o_ps[i % 2][:, :], v[s_][:, j, :], pT[m_][:, m % 4, :],
                                                 start=(j == 0 and k == 0), stop=(j == i and k == 2))
                            last.then_inc(pv_done.sem, 1)
                        for t in WO_AFTER.get(m, []):
                            if t == 0:
                                pe.wait_ge(w_lo[1].sem, w_lo[1].at("a", b, g, CHUNKS[1]["a"]))
                            pe.wait_ge(o_free.sem, o_free.at("a", b, g, t + 1))
                            pe.wait_ge(y_free.sem, y_free.at("a", b, g, t - 1))
                            product(y_ps[t % 2][:, :],
                                    [([oT[s_][:, h, t * P:(t + 1) * P] for s_ in range(2)],
                                      [wo(W[m_], h) for m_ in range(2)]) for h in range(HG)]).then_inc(y.sem, 1)
                front("b", b)
                with pe.Fori(0, NQ) as g:
                    pe.wait_ge(proj_free.sem, proj_free.at("b", b, g, 0))
                    pe.wait_ge(w_lo[0].sem, w_lo[0].at("b", b, g, CHUNKS[0]["b"]))
                    for m in range(IC):
                        for w, ps, free, done in ((wup, score_ps, h_f, score), (wgate, proj_ps, proj_free, proj)):
                            pe.wait_ge(free.sem, free.at("b", b, g, m - 1))
                            product(ps[m % 2][:, :],
                                    [([w(W[s_], c, m) for s_ in range(2)], [XnT[m_][:, c, :] for m_ in range(2)])
                                     for c in range(KD)]).then_inc(done.sem, 1)
                    pe.wait_ge(w_lo[1].sem, w_lo[1].at("b", b, g, CHUNKS[1]["b"]))

                    def hidden_ready(m):
                        pe.wait_ge(h_lo.sem, h_lo.at("b", b, g, m + 1))

                    for t in range(NT):
                        pe.wait_ge(y_free.sem, y_free.at("b", b, g, t - 1))
                        product(y_ps[t % 2][:, :],
                                [([hT[s_][:, m, t * P:(t + 1) * P] for s_ in range(2)],
                                  [wo(W[m_], m) for m_ in range(2)]) for m in range(IC)],
                                hidden_ready if t == 0 else lambda m: None).then_inc(y.sem, 1)
                front("c", b)
                pe.wait_ge(proj_free.sem, proj_free.at("front_c", b, None, NT))
                pe.wait_ge(w_lo[0].sem, w_lo[0].at("c", b, None, CHUNKS[0]["c"]))

                def packs(t):
                    pe.wait_ge(rot_lo.sem, rot_lo.at("c", b, None, 2 * t + 2))
                    for u in range(6):
                        pe.wait_ge(moved[u % 2].sem, moved[u % 2].at("c", b, None, 3 * t + u // 2))
                        for n in range(4):
                            src = q_pack[:, 2 * (4 * u + n):2 * (4 * u + n) + 2, :].rearrange("p h d -> p (h d)") if u < 4 \
                                else k_pack[:, 4 * (u - 4) + n, :, :].rearrange("p a d -> p (a d)")
                            last = pe.transpose(score_ps[u % 2][:, n * P:(n + 1) * P], src.bitcast(F32), ident[:, :])
                        last.then_inc(score.sem, 1)

                for t in range(NT):
                    for part, w in enumerate((wq1, wkv1)):
                        width = w(W[0], 0).shape[1]
                        pe.wait_ge(proj_free.sem, proj_free.at("qkv", b, None, 2 * t + part - 1))
                        product(proj_ps[part][:, 0:width],
                                [([XnT[s_][:, c, t * P:(t + 1) * P] for s_ in range(2)], [w(W[m_], c) for m_ in range(2)])
                                 for c in range(KD)]).then_inc(proj.sem, 1)
                    if t >= 1:
                        packs(t - 1)
                packs(NT - 1)
                for n in range(2):
                    pe.wait_ge(moved[n].sem, moved[n].at("c", b, None, 3 * NT))

                def scores(k, u):
                    i, heads = S1_BANKS[u]
                    w, n = (i + 1) * P, k * NS + u
                    ps = score_ps[n % 2]
                    pe.wait_ge(s_max.sem, s_max.at("c", b, None, n - 1))
                    for m, (q, pair) in enumerate(heads):
                        rows = slice(64 * q, 64 * q + 64)
                        pe.matmul(ps[:, m * w:(m + 1) * w], QT[rows, 2 * k + pair, i * P:(i + 1) * P], KT[rows, k, 0:w],
                                  start=(m == 0), stop=False, skip_group_check=True)
                    dst = ps[:, 0:len(heads) * w].rearrange("p (h s) -> p h s", s=w)[:, :, i * P:w]
                    pe.matmul(dst, ident_b[:, :], mask[:, :].unsqueeze(1).to_broadcast([P, len(heads), P]),
                              start=False, stop=True, skip_group_check=True).then_inc(score.sem, 1)

                def scores_T(g, u):
                    j, heads = S2_BANKS[u]
                    w, n = S - j * P, g * NS + u
                    if u == 0:
                        pe.wait_ge(m_in.sem, m_in.at("c", b, None, 32 * (g + 1)))
                    pe.wait_ge(proj_free.sem, proj_free.at("s2", b, None, n - 1))
                    for m, (q, pair) in enumerate(heads):
                        rows = slice(64 * q, 64 * q + 64)
                        last = pe.matmul(proj_ps[n % 2][:, m * w:(m + 1) * w], KT[rows, g, j * P:(j + 1) * P],
                                         QT[rows, 2 * g + pair, j * P:S], start=True, stop=True)
                    last.then_inc(proj.sem, 1)

                def values(g, j):
                    if j == 0:
                        pe.wait_ge(yT_done.sem, yT_done.at("c", b, None, g - 1))
                    pe.wait_ge(masked.sem, masked.at("c", b, None, g * NT + j + 1))
                    for m, (q, pair) in enumerate(HEADS1):
                        at = 32 * (2 * pair + q)
                        last = pe.matmul(o_ps[g % 2][at:at + 32, j * P:S], V1[:, j, g, :], probs[j][:, m, :],
                                         start=(j == 0), stop=(j == NT - 1), skip_group_check=True)
                    last.then_inc(pv1.sem, 1)

                for k in range(KV1 + 3):
                    for u in range(NS):
                        if k < KV1:
                            scores(k, u)
                        g = k - 1
                        if u == 1 and 0 <= g < KV1:
                            pe.wait_ge(s_max.sem, s_max.at("c", b, None, (g + 1) * NS))
                            pe.wait_ge(maxT_done.sem, maxT_done.at("c", b, None, g)) if g >= 1 else None
                            for i in range(NT):
                                last = pe.matmul(y_ps[0][0:4, i * P:(i + 1) * P],
                                                 row_max[:, g, i, :, :].rearrange("p q n -> p (q n)"), ident[:, :],
                                                 start=True, stop=True)
                            last.then_inc(max_rows.sem, 1)
                        g = k - 2
                        if 0 <= g < KV1:
                            scores_T(g, u)
                            if u == 6:
                                values(g, 0)
                            if u == 9:
                                values(g, 1)
                        g = k - 3
                        if g >= 0:
                            if u == 0:
                                values(g, 2)
                            if u == 2:
                                values(g, 3)
                            if u == 5:
                                pe.wait_ge(yT_done.sem, yT_done.at("c", b, None, g + 1))
                                pe.wait_ge(y1_done.sem, y1_done.at("c", b, None, g))
                                for i in range(NT):
                                    last = pe.transpose(y_ps[1][:, i * P:(i + 1) * P], yT[:, g % 2, i * P:(i + 1) * P],
                                                        ident[:, :])
                                last.then_inc(y_back.sem, 1)
                front("y", b)
                pe.wait_ge(proj_free.sem, proj_free.at("front_y", b, None, NT))
                pe.wait_ge(w_lo[1].sem, w_lo[1].at("c", b, None, CHUNKS[1]["c"]))
                for t in range(NT):
                    pe.wait_ge(y_free.sem, y_free.at("c", b, None, t - 1))
                    product(y_ps[t % 2][:, :],
                            [([XnT[s_][:, c, t * P:(t + 1) * P] for s_ in range(2)], [wo(W[m_], c) for m_ in range(2)])
                             for c in range(KD)]).then_inc(y.sem, 1)
                front("d", b)
                pe.wait_ge(proj_free.sem, proj_free.at("front_d", b, None, NT))
                pe.wait_ge(w_lo[0].sem, w_lo[0].at("d", b, None, CHUNKS[0]["d"]))
                for t in range(NT):
                    pe.wait_ge(y_free.sem, y_free.at("d", b, None, t - 1))
                    product(y_ps[t % 2][:, :],
                            [([XnT[s_][:, c, t * P:(t + 1) * P] for s_ in range(2)],
                              [W[m_][:, c * D:(c + 1) * D] for m_ in range(2)]) for c in range(KD)]).then_inc(y.sem, 1)

            def rows_T(stage, g, src, k):
                pe.wait_ge(row.sem, row.at(stage, 0, g, k))
                for c in range(KD):
                    last = pe.matmul(o_ps[0][:, c * R:(c + 1) * R], src[:, c * P:(c + 1) * P], ident[0:R, 0:R],
                                     start=True, stop=True)
                last.then_inc(row_mm.sem, 1)
                pe.wait_ge(row.sem, row.at(stage, 0, g, k + 1))

            def linear(w):
                for c in range(KD):
                    last = pe.matmul(o_ps[1][0:R, :], rowsT[:, c, :], w[:, c, :], start=(c == 0), stop=(c == KD - 1))
                last.then_inc(row_mm.sem, 1)

            rows_T("pre", None, rows, 8)
            linear(aggw)
            with pe.Fori(0, K_STEPS) as g:
                rows_T("step", g, rows, 5)
                for c in range(KD):
                    for n in range(4):
                        last = pe.matmul(score_ps[0][R * n:R * n + R, :], rowsT[:, c, :], d1w[:, c, n * D:(n + 1) * D],
                                         start=(c == 0), stop=(c == KD - 1), skip_group_check=True)
                last.then_inc(row_mm.sem, 1)
                pe.wait_ge(gelu_done.sem, gelu_done.at("step", 0, g, 1))
                for c in range(KD):
                    last = pe.transpose(score_ps[1][:, c * P:(c + 1) * P], hidden[:, c * P:(c + 1) * P], ident[:, :])
                last.then_inc(row_mm.sem, 1)
                pe.wait_ge(row.sem, row.at("step", 0, g, 8))
                for c in range(KD):
                    for n in range(4):
                        last = pe.matmul(proj_ps[0][R * n:R * n + R, :], hiddenT[:, c, R * n:R * n + R], d2w[:, n * KD + c, :],
                                         start=(c == 0), stop=(c == KD - 1), skip_group_check=True)
                last.then_inc(row_mm.sem, 1)
                pe.wait_ge(row.sem, row.at("step", 0, g, 9))
                pe.matmul(proj_ps[1][0:R, :], summing[:, :], partial, start=True, stop=True).then_inc(row_mm.sem, 1)
            rows_T("post", None, thought, 0)
            linear(bcw)


def rope0_tables():
    import numpy as np
    inv = np.float32(1) / np.float32(10000) ** (np.arange(0, DH0, 2, dtype=np.float32) / np.float32(DH0))
    ang = (np.arange(S, dtype=np.float32)[:, None] * inv[None, :].astype(np.float32)).T
    cos, sin = np.cos(ang), np.sin(ang)
    return (np.concatenate([cos, cos]).astype(np.float32), np.concatenate([-sin, sin]).astype(np.float32))


def rope1_table():
    import numpy as np
    inv = np.float32(1) / np.float32(10000) ** (np.arange(0, HD1, 2, dtype=np.float32) / np.float32(HD1))
    ang = np.arange(S, dtype=np.float32)[:, None] * inv[None, :].astype(np.float32)
    cos = np.repeat(np.cos(ang), 2, axis=1)
    sin = np.stack([-np.sin(ang), np.sin(ang)], axis=2).reshape(S, HD1)
    scale = np.float32(HD1 ** -0.5)
    t = np.stack([cos * scale, sin * scale, cos, sin]).reshape(4, NT, P, HD1).transpose(2, 0, 1, 3)
    return np.ascontiguousarray(t.reshape(P, 4 * NT * HD1).astype(np.float32))


def decay_table():
    import numpy as np
    lam = np.exp2(np.float32(-8) * np.arange(1, H0 + 1, dtype=np.float32) / np.float32(H0)).astype(np.float32)
    diff = (np.arange(NT)[:, None] * P + np.arange(P)[None, :])[None] - np.arange(P)[:, None, None]
    diff = diff.astype(np.float32)
    t = np.where(diff[None] >= 0, np.exp(-lam[:, None, None, None] * np.maximum(diff[None], 0)), 0)
    t = t.reshape(KV0, HG, P, NT, P).transpose(0, 2, 1, 3, 4)
    return np.ascontiguousarray(t.reshape(KV0, P, HG * NT * P).astype(np.float32))


def kernel(**inputs):
    import ml_dtypes
    import numpy as np
    import concourse.bacc as bacc
    from concourse.bass_utils import run_bass_kernel_spmd

    a = {k: np.asarray(v) for k, v in inputs.items()}

    def rows(w, n, per):
        return w.reshape(n, per, KD, P).transpose(0, 3, 2, 1).reshape(n, P, KD * per)

    def cols(w, n):
        k = w.shape[1] // n // P
        return w.T.reshape(n, k, P, w.shape[0]).transpose(0, 2, 1, 3).reshape(n, P, k * w.shape[0])

    def blocks(w):
        return w.reshape(-1, P, w.shape[1]).transpose(1, 0, 2)

    cos0, sin0 = rope0_tables()
    arrays = {
        "x": a["L0_attn_x"],
        "w_a": np.concatenate([rows(a["L0_attn_wk"], KV0, P), rows(a["L0_attn_wv"], KV0, P),
                               rows(a["L0_attn_wq"], KV0, HG * P), cols(a["L0_attn_wo"], KV0)], axis=2),
        "w_b": np.concatenate([rows(a["L0_ffn_up_w"], NQ, I0 // NQ), rows(a["L0_ffn_gate_w"], NQ, I0 // NQ),
                               cols(a["L0_ffn_down_w"], NQ)], axis=2),
        "gate_scale": a["L0_ffn_gate_scale"].reshape(I0 // P, P).T,
        "up_scale": a["L0_ffn_up_scale"].reshape(I0 // P, P).T,
        "down_scale": a["L0_ffn_down_scale"],
        "rope0_cos": cos0, "rope0_sin": sin0, "decay": decay_table(),
        "identity": np.eye(P, dtype=np.float32),
        "w_c": np.concatenate([
            np.concatenate([rows(a["L1_attn_wk"], 1, P).reshape(P, KD, P),
                            rows(a["L1_attn_wv"], 1, P).reshape(P, KD, P)], axis=2).reshape(1, P, KD * 2 * P),
            rows(a["L1_attn_wq"], 1, D), cols(a["L1_attn_wo"], 1)], axis=2),
        "rope1_tables": rope1_table(),
        "w_gate": blocks(a["L1_ffn_gate_w"]).reshape(P, KD * D), "agg_w": blocks(a["L1_ffn_agg_w"]),
        "bc_w": blocks(a["L1_ffn_bc_w"]), "d1_w": blocks(a["L1_ffn_d1_w"]), "d2_w": blocks(a["L1_ffn_d2_w"]),
        **{n: a["L1_ffn_" + n] for n in ("gate_b", "in_gamma", "in_beta", "agg_b", "pn_gamma", "pn_beta", "d1_b",
                                         "d2_b", "bc_b", "out_gamma", "out_beta")},
        "row_sum": np.tile(np.eye(R, dtype=np.float32), (P // R, 1)),
        "causal": np.triu(np.full((P, P), MASKED, np.float32), 1).astype(ml_dtypes.bfloat16),
        "identity_b": np.eye(P, dtype=np.float32).astype(ml_dtypes.bfloat16),
    }
    arrays = {k: np.ascontiguousarray(v) for k, v in arrays.items()}
    nc = bacc.Bacc("TRN2", target_bir_lowering=False, num_devices=1)
    args = {k: nc.dram_tensor(k, v.shape, mybir.dt.from_np(v.dtype), kind="ExternalInput").ap()
            for k, v in arrays.items()}
    out = nc.dram_tensor("out", arrays["x"].shape, F32, kind="ExternalOutput").ap()
    build(nc, out=out, **args)
    r = run_bass_kernel_spmd(nc, [arrays], core_ids=[0])
    return r.results[0]["out"]
```
